# Optimizing a Trainium2 kernel written in Bass

```python
import numpy as np
import jax
import jax.numpy as jnp

def _softmax(x, axis=-1):
    return jax.nn.softmax(x, axis=axis)

def _gelu(x):
    return jax.nn.gelu(x, approximate=True)

def _silu(x):
    return jax.nn.silu(x)

def _sigmoid(x):
    return jax.nn.sigmoid(x)

def _layernorm(x, axis=-1, eps=1e-05):
    m = jnp.mean(x, axis=axis, keepdims=True)
    v = jnp.var(x, axis=axis, keepdims=True)
    return (x - m) / jnp.sqrt(v + eps)

def _scatter_add(tgt, idx, src, axis=0):
    return tgt.at[idx].add(src)

def _segment_sum(src, seg, n):
    return jax.ops.segment_sum(src, seg, n)
kernel_name = 'mk_macaron_d1_jaxref_r8_8e0497'

def setup_inputs(seed: int=0):
    np.random.seed(seed)
    _w = jnp.asarray

    def _L0_attn_setup():
        import jax, jax.numpy as jnp
        import numpy as np
        D_HEAD = 64
        MASK_FILL = -1000000.0
        key = jax.random.key(seed)
        ks = jax.random.split(key, 5)
        batch, seq, d_model, n_heads, d_head = (4, 256, 128, 16, D_HEAD)
        bound_qkv = float(np.sqrt(6.0 / (d_model + n_heads * d_head)))
        bound_out = float(np.sqrt(6.0 / (d_head + n_heads * d_model)))
        return {'resid': jax.random.normal(ks[0], (batch, seq, d_model), dtype=jnp.float32), 'W_Q': jax.random.uniform(ks[1], (d_model, n_heads, d_head), jnp.float32, -bound_qkv, bound_qkv), 'W_K': jax.random.uniform(ks[2], (d_model, n_heads, d_head), jnp.float32, -bound_qkv, bound_qkv), 'W_V': jax.random.uniform(ks[3], (d_model, n_heads, d_head), jnp.float32, -bound_qkv, bound_qkv), 'W_out': jax.random.uniform(ks[4], (d_head, n_heads, d_model), jnp.float32, -bound_out, bound_out), 'b_out': jnp.zeros((d_model,), dtype=jnp.float32)}
    _L0_attn_in = _L0_attn_setup()

    def _L0_ffn_setup():
        import jax, jax.numpy as jnp
        import numpy as np
        B, S, H = (2, 256, 128)
        F = 512
        E = 8
        TOP_K = 2
        SHARED_SCALE = 0.1
        EPS = 1e-09

        def _moe_forward(x3, Wg, W1, b1, W2, b2, Ws1, bs1, Ws2, bs2):
            b, s, h = x3.shape
            x = x3.reshape(-1, h)
            T = x.shape[0]
            logits = x @ Wg
            probs = jax.nn.softmax(logits, axis=-1)
            vals, idx = jax.lax.top_k(probs, TOP_K)
            weights = vals / (jnp.sum(vals, axis=-1, keepdims=True) + EPS)
            cw = jnp.zeros((T, E), dtype=x.dtype).at[jnp.arange(T)[:, None], idx].set(weights)
            hpre = jnp.einsum('th,ehf->tef', x, W1) + b1
            act = jax.nn.silu(hpre)
            y = jnp.einsum('tef,efh->teh', act, W2) + b2
            out = jnp.einsum('te,teh->th', cw, y)
            shared = jax.nn.silu(x @ Ws1 + bs1) @ Ws2 + bs2
            out = out + SHARED_SCALE * shared
            return out.reshape(b, s, h)
        key = jax.random.key(seed)
        ks = jax.random.split(key, 10)
        sc = 0.02
        return {'hidden_states': jax.random.normal(ks[0], (B, S, H), dtype=jnp.float32), 'Wg': jax.random.normal(ks[1], (H, E), dtype=jnp.float32) * sc, 'W1': jax.random.normal(ks[2], (E, H, F), dtype=jnp.float32) * sc, 'b1': jnp.zeros((E, F), dtype=jnp.float32), 'W2': jax.random.normal(ks[3], (E, F, H), dtype=jnp.float32) * sc, 'b2': jnp.zeros((E, H), dtype=jnp.float32), 'Ws1': jax.random.normal(ks[4], (H, F), dtype=jnp.float32) * sc, 'bs1': jnp.zeros((F,), dtype=jnp.float32), 'Ws2': jax.random.normal(ks[5], (F, H), dtype=jnp.float32) * sc, 'bs2': jnp.zeros((H,), dtype=jnp.float32)}
    _L0_ffn_in = _L0_ffn_setup()
    _d = {'L0_attn_resid': _L0_attn_in['resid'], 'L0_attn_W_Q': _L0_attn_in['W_Q'], 'L0_attn_W_K': _L0_attn_in['W_K'], 'L0_attn_W_V': _L0_attn_in['W_V'], 'L0_attn_W_out': _L0_attn_in['W_out'], 'L0_attn_b_out': _L0_attn_in['b_out'], 'L0_ffn_Wg': _L0_ffn_in['Wg'], 'L0_ffn_W1': _L0_ffn_in['W1'], 'L0_ffn_b1': _L0_ffn_in['b1'], 'L0_ffn_W2': _L0_ffn_in['W2'], 'L0_ffn_b2': _L0_ffn_in['b2'], 'L0_ffn_Ws1': _L0_ffn_in['Ws1'], 'L0_ffn_bs1': _L0_ffn_in['bs1'], 'L0_ffn_Ws2': _L0_ffn_in['Ws2'], 'L0_ffn_bs2': _L0_ffn_in['bs2']}
    _x0 = _d['L0_attn_resid']
    _d['L0_attn_resid'] = jax.random.normal(jax.random.fold_in(jax.random.key(seed), 1), (4, 1024, 128), dtype=_x0.dtype)
    del _x0
    return _d

def reference(L0_attn_resid, L0_attn_W_Q, L0_attn_W_K, L0_attn_W_V, L0_attn_W_out, L0_attn_b_out, L0_ffn_Wg, L0_ffn_W1, L0_ffn_b1, L0_ffn_W2, L0_ffn_b2, L0_ffn_Ws1, L0_ffn_bs1, L0_ffn_Ws2, L0_ffn_bs2):

    def _L0_attn_ref(resid, W_Q, W_K, W_V, W_out, b_out):
        import jax, jax.numpy as jnp
        import numpy as np
        D_HEAD = 64
        MASK_FILL = -1000000.0
        seq = resid.shape[1]
        d_head = W_Q.shape[-1]
        q = jnp.einsum('bsd,dhk->bshk', resid, W_Q)
        k = jnp.einsum('bsd,dhk->bshk', resid, W_K)
        v = jnp.einsum('bsd,dhk->bshk', resid, W_V)
        scores = jnp.einsum('bqhk,bkhd->bhqd', q, k.astype(q.dtype)) if False else jnp.einsum('bqhc,bshc->bhqs', q, k)
        scores = scores / jnp.sqrt(jnp.asarray(d_head, dtype=scores.dtype))
        causal_mask = jnp.triu(jnp.ones((seq, seq), dtype=bool), k=1)
        scores = jnp.where(causal_mask, MASK_FILL, scores)
        probs = jax.nn.softmax(scores, axis=-1)
        z = jnp.einsum('bhqs,bshc->bqhc', probs, v)
        out = jnp.einsum('bqhc,chd->bqd', z, W_out) + b_out
        return out

    def _L0_ffn_ref(hidden_states, Wg, W1, b1, W2, b2, Ws1, bs1, Ws2, bs2):
        import jax, jax.numpy as jnp
        import numpy as np
        B, S, H = (2, 256, 128)
        F = 512
        E = 8
        TOP_K = 2
        SHARED_SCALE = 0.1
        EPS = 1e-09

        def _moe_forward(x3, Wg, W1, b1, W2, b2, Ws1, bs1, Ws2, bs2):
            b, s, h = x3.shape
            x = x3.reshape(-1, h)
            T = x.shape[0]
            logits = x @ Wg
            probs = jax.nn.softmax(logits, axis=-1)
            vals, idx = jax.lax.top_k(probs, TOP_K)
            weights = vals / (jnp.sum(vals, axis=-1, keepdims=True) + EPS)
            cw = jnp.zeros((T, E), dtype=x.dtype).at[jnp.arange(T)[:, None], idx].set(weights)
            hpre = jnp.einsum('th,ehf->tef', x, W1) + b1
            act = jax.nn.silu(hpre)
            y = jnp.einsum('tef,efh->teh', act, W2) + b2
            out = jnp.einsum('te,teh->th', cw, y)
            shared = jax.nn.silu(x @ Ws1 + bs1) @ Ws2 + bs2
            out = out + SHARED_SCALE * shared
            return out.reshape(b, s, h)
        return _moe_forward(hidden_states, Wg, W1, b1, W2, b2, Ws1, bs1, Ws2, bs2)
    x = L0_attn_resid
    x = x + 0.5 * _L0_ffn_ref(_layernorm(x, axis=-1), L0_ffn_Wg, L0_ffn_W1, L0_ffn_b1, L0_ffn_W2, L0_ffn_b2, L0_ffn_Ws1, L0_ffn_bs1, L0_ffn_Ws2, L0_ffn_bs2)
    x = x + _L0_attn_ref(_layernorm(x, axis=-1), L0_attn_W_Q, L0_attn_W_K, L0_attn_W_V, L0_attn_W_out, L0_attn_b_out)
    x = x + 0.5 * _L0_ffn_ref(_layernorm(x, axis=-1), L0_ffn_Wg, L0_ffn_W1, L0_ffn_b1, L0_ffn_W2, L0_ffn_b2, L0_ffn_Ws1, L0_ffn_bs1, L0_ffn_Ws2, L0_ffn_bs2)
    return x

_drawn_inputs = setup_inputs


def setup_inputs(seed=0):
    import zlib

    import numpy as np

    out = dict(_drawn_inputs(seed))
    spreads = {'L0_attn_b_out': (0.0, 0.1),
     'L0_ffn_b1': (0.0, 0.491),
     'L0_ffn_b2': (0.0, 0.1),
     'L0_ffn_bs1': (0.0, 0.8),
     'L0_ffn_bs2': (0.0, 0.747)}
    factors = {'L0_attn_W_Q': 4.508, 'L0_attn_W_K': 4.541, 'L0_ffn_Ws1': 8.0, 'L0_ffn_Ws2': 8.0}
    for name, (base, spread) in spreads.items():
        noise = np.random.default_rng([zlib.crc32(name.encode()), seed]).standard_normal(out[name].shape)
        drawn = base * np.exp(spread * noise) if base else spread * noise
        out[name] = jnp.asarray(drawn.astype(out[name].dtype))
    for name, factor in factors.items():
        out[name] = (out[name] * factor).astype(out[name].dtype)
    return out
```

```python
from contextlib import ExitStack

import concourse.bass as bass
from concourse import mybir

F32 = mybir.dt.float32
F32R = mybir.dt.float32r
BF16 = mybir.dt.bfloat16
ALU = mybir.AluOpType
ACT = mybir.ActivationFunctionType
AX_X = mybir.AxisListType.X

P = 128
LO = 32
CH = 512
LN_EPS = 1e-5
TOPK_EPS = 1e-9
SHARED_SCALE = 0.1
HALF = 0.5
NEG = -1e30


def f32(ap):
    return ap.bitcast(F32)


def pool_copy(nc, g, out, in_, p0=0):
    shape = list(in_.shape)
    one = g.ones[p0:p0 + shape[0], 0:1]
    for k in range(len(shape) - 2):
        one = one.unsqueeze(1)
    return nc.gpsimd.tensor_tensor(out, in_, one.to_broadcast(shape), ALU.mult)


def give(eng, *sems):
    for sem in sems:
        eng.sem_inc(sem, 1)


class Ctx:

    def __init__(self, nc, stack):
        self.nc, self.stack, self.n = nc, stack, 0

    def sb(self, name, shape, dt=F32):
        return self.stack.enter_context(self.nc.sbuf_tensor(f"{name}_{self.n}", shape, dt))

    def ps(self, name, shape, dt=F32):
        return self.stack.enter_context(self.nc.psum_tensor(f"{name}_{self.n}", shape, dt))

    def sem(self, name):
        return self.stack.enter_context(self.nc.semaphore(f"{name}_{self.n}"))


def load_constants(nc, g, x):
    with ExitStack() as st:
        c = Ctx(nc, st)
        loaded, zeroed, made = c.sem("c_loaded"), c.sem("c_zeroed"), c.sem("c_made")
        block = st.enter_context(nc.Block())
        T = g.resid.shape[1]

        @block.sync
        def _(sp):
            sp.dma_start(g.resid[:], x.rearrange("b (t p) d -> p (b t) d", p=P)).then_inc(loaded, 16)
            sp.wait_ge(loaded, 16)

        @block.vector
        def _(dve):
            nc.vector.memset(g.ident[:], 0.0)
            nc.vector.memset(g.ident_b[:], 0.0)
            nc.vector.memset(g.mask_keys[:], 0.0)
            nc.vector.memset(g.mask_queries[:], 0.0)
            nc.vector.memset(g.ones[:], 1.0)
            nc.vector.memset(g.eps[:], LN_EPS)
            nc.vector.memset(f32(g.select[:]), 0.0).then_inc(zeroed, 1)

        @block.gpsimd
        def _(pool):
            pool.wait_ge(zeroed, 1)
            diag = dict(compare_op=ALU.not_equal, fill=1.0, base=0, pattern=[[-1, P]], channel_multiplier=1)
            nc.gpsimd.affine_select(out=g.ident[:], in_=g.ident[:], **diag)
            nc.gpsimd.affine_select(out=g.ident_b[:], in_=g.ident_b[:], **diag)
            nc.gpsimd.affine_select(out=g.mask_keys[:], in_=g.mask_keys[:], compare_op=ALU.is_ge, fill=NEG,
                                    base=0, pattern=[[-1, P]], channel_multiplier=1)
            nc.gpsimd.affine_select(out=g.mask_queries[:], in_=g.mask_queries[:], compare_op=ALU.is_ge,
                                    fill=NEG, base=0, pattern=[[1, P]], channel_multiplier=-1)
            E = g.select.shape[1]
            for k, first in enumerate((0, LO)):
                nc.gpsimd.affine_select(out=g.select[:], in_=f32(g.select[:]), compare_op=ALU.not_equal, fill=1.0,
                                        base=-first, pattern=[[-1, E], [0, P]], channel_multiplier=1).then_inc(made, 1)
                pool.wait_ge(made, k + 1)
            nc.gpsimd.iota(g.rank_i[:], pattern=[[-1, E]], base=E, channel_multiplier=0).then_inc(made, 1)
            pool.wait_ge(made, 3)
            nc.gpsimd.tensor_copy(g.rank[:], g.rank_i[:]).then_inc(made, 1)


def layernorm(nc, g, wg):
    with ExitStack() as st:
        c = Ctx(nc, st)
        c.n = g.stage
        T = g.resid.shape[1]
        GT = CH // P
        G = T // GT
        E = g.select.shape[1]
        stats = c.sb("stats", [P, T, 6])
        moments = c.sb("moments", [P, T, 2])
        std = c.sb("std", [P, T])
        rstd = c.sb("rstd", [P, T])
        xn = [c.sb(f"xn{s}", [P, GT, P]) for s in range(2)]
        xT = [c.ps(f"xT{s}", [P, CH]) for s in range(2)]
        stats_done, moments_done, std_done, rstd_done = (c.sem(x) for x in ("stats", "mom", "std", "rstd"))
        xn_ready, xT_ready, hi_ready, lo_ready = (c.sem(x) for x in ("xn_r", "xT_r", "hi_r", "lo_r"))
        if wg is not None:
            wg_raw = c.sb("wg_raw", [P, E])
            wgh = c.sb("wgh", [P, E], F32R)
            wgl = c.sb("wgl", [P, E], F32R)
            lgT_sb = [c.sb(f"lgT_sb{s}", [E, CH]) for s in range(2)]
            lgT = [c.ps(f"lgT{s}", [E, CH]) for s in range(2)]
            lg = [c.ps(f"lg{s}", [P, GT * E]) for s in range(2)]
            logits = c.sb("logits", [P, T, E])
            work = [c.sb(f"work{s}", [P, T, E]) for s in range(6)]
            col = [c.sb(f"col{s}", [P, T]) for s in range(10)]
            wg_loaded, wg_split = c.sem("wg_l"), c.sem("wg_s")
            lgT_ready, lgT_copied, lg_ready, lg_copied = (c.sem(x) for x in ("lgT_r", "lgT_c", "lg_r", "lg_c"))
            chain, z_ready, exp_ready, cw_ready = (c.sem(x) for x in ("chain", "z_r", "exp_r", "cw_r"))
            cwT_ready, cwh_ready, cwl_ready, cw_zeroed = (c.sem(x) for x in ("cwT_r", "cwh_r", "cwl_r", "cw_z"))
        block = st.enter_context(nc.Block())

        if wg is not None:
            @block.sync
            def _(sp):
                sp.dma_start(wg_raw[:], wg).then_inc(wg_loaded, 16)

        @block.vector
        def _(dve):
            give(dve, lo_ready)
            if wg is not None:
                give(dve, lg_copied)
            with dve.Fori(0, T // 4) as q:
                for j in range(4):
                    t = q * 4
                    nc.vector.bn_stats(stats[:, bass.ds(t + j, 1), :], g.resid[:, bass.ds(t + j, 1), :]).then_inc(stats_done, 1)
            dve.wait_ge(stats_done, T)
            for t in range(T):
                last = nc.vector.bn_aggr(moments[:, t, :], stats[:, t, :])
            last.then_inc(moments_done, 1)
            dve.wait_ge(std_done, 1)
            nc.vector.reciprocal(rstd[:], std[:]).then_inc(rstd_done, 1)
            dve.wait_ge(rstd_done, 1)
            if wg is not None:
                nc.vector.memset(f32(g.cwT[:]), 0.0).then_inc(cw_zeroed, 1)
                dve.wait_ge(wg_loaded, 16)
                nc.vector.tensor_copy(wgh[:], wg_raw[:]).then_inc(wg_split, 1)
                dve.wait_ge(wg_split, 1)
                nc.vector.tensor_tensor(wgl[:], wg_raw[:], f32(wgh[:]), ALU.subtract).then_inc(wg_split, 1)
            with dve.Fori(0, G // 2) as i:
                for s in range(2):
                    dve.wait_ge(xT_ready, i * 2 + 1)
                    for j in range(GT):
                        k = i * (2 * GT) + (s * GT + j)
                        last = nc.vector.tensor_scalar(
                            xn[s][:, j, :], g.resid[:, bass.ds(k, 1), :], moments[:, bass.ds(k, 1), 0:1],
                            rstd[:, bass.ds(k, 1)], ALU.subtract, ALU.mult)
                    last.then_inc(xn_ready, 1)
                for s in range(2):
                    dve.wait_ge(hi_ready, i * 2 + (s + 1))
                    at = bass.ds(i * (2 * CH) + s * CH, CH)
                    nc.vector.tensor_tensor(g.xl[:, at], xT[s][:], f32(g.xh[:, at]), ALU.subtract).then_inc(lo_ready, 1)
                if wg is not None:
                    for s in range(2):
                        dve.wait_ge(lg_ready, i * 2 + (s + 1))
                        nc.vector.tensor_copy(
                            logits[:, bass.ds(i * (2 * GT) + s * GT, GT), :],
                            lg[s][:].rearrange("p (t e) -> p t e", e=E)).then_inc(lg_copied, 1)
            if wg is None:
                return

            n = [0]

            def link(ins):
                n[0] += 1
                ins.then_inc(chain, 1)
                dve.wait_ge(chain, n[0])

            def over(a):
                return a[:].unsqueeze(2).to_broadcast([P, T, E])

            tt, red = nc.vector.tensor_tensor, nc.vector.tensor_reduce
            rank = g.rank[:].unsqueeze(1).to_broadcast([P, T, E])
            z, e, w2, eq, s1, s2 = work
            mx, se, rs, v1, k1, v2, k2, den, rden, _ = col
            dve.wait_ge(lg_copied, G + 1)
            link(red(mx[:], logits[:], AX_X, ALU.max))
            tt(z[:], logits[:], over(mx), ALU.subtract).then_inc(z_ready, 1)
            dve.wait_ge(exp_ready, 1)
            link(red(se[:], e[:], AX_X, ALU.add))
            link(nc.vector.reciprocal(rs[:], se[:]))
            link(tt(z[:], e[:], over(rs), ALU.mult))
            link(red(v1[:], z[:], AX_X, ALU.max))
            link(tt(eq[:], z[:], over(v1), ALU.is_equal))
            link(tt(w2[:], eq[:], rank, ALU.mult))
            link(red(k1[:], w2[:], AX_X, ALU.max))
            link(tt(s1[:], w2[:], over(k1), ALU.is_equal))
            link(nc.vector.scalar_tensor_tensor(eq[:], s1[:], -2.0, z[:], ALU.mult, ALU.add))
            link(red(v2[:], eq[:], AX_X, ALU.max))
            link(tt(w2[:], eq[:], over(v2), ALU.is_equal))
            link(tt(eq[:], w2[:], rank, ALU.mult))
            link(red(k2[:], eq[:], AX_X, ALU.max))
            link(tt(s2[:], eq[:], over(k2), ALU.is_equal))
            link(tt(den[:], v1[:], v2[:], ALU.add))
            link(nc.vector.tensor_scalar(se[:], den[:], TOPK_EPS, None, ALU.add))
            link(nc.vector.reciprocal(rden[:], se[:]))
            link(nc.vector.tensor_scalar(den[:], rden[:], HALF, None, ALU.mult))
            link(tt(w2[:], s1[:], s2[:], ALU.add))
            link(tt(eq[:], w2[:], z[:], ALU.mult))
            tt(w2[:], eq[:], over(den), ALU.mult).then_inc(cw_ready, 1)
            for q in range(G):
                dve.wait_ge(cwh_ready, q + 1)
                at = slice(q * CH, (q + 1) * CH)
                nc.vector.tensor_tensor(g.cwT[LO:LO + E, at], lgT[q % 2][:], f32(g.cwT[0:E, at]), ALU.subtract).then_inc(cwl_ready, 1)

        @block.scalar
        def _(act):
            act.wait_ge(moments_done, 1)
            nc.scalar.activation(std[:], moments[:, :, 1], ACT.Sqrt, bias=g.eps[:]).then_inc(std_done, 1)
            with act.Fori(0, G // 2) as i:
                for s in range(2):
                    act.wait_ge(xT_ready, i * 2 + (s + 1) + 1)
                    nc.scalar.activation(g.xh[:, bass.ds(i * (2 * CH) + s * CH, CH)], xT[s][:], ACT.Copy).then_inc(hi_ready, 1)
                if wg is not None:
                    for s in range(2):
                        act.wait_ge(lgT_ready, i * 2 + (s + 1))
                        nc.scalar.activation(lgT_sb[s][:], lgT[s][:], ACT.Copy).then_inc(lgT_copied, 1)
            if wg is None:
                return
            act.wait_ge(z_ready, 1)
            act.wait_ge(cw_zeroed, 1)
            nc.scalar.activation(work[1][:], work[0][:], ACT.Exp).then_inc(exp_ready, 1)
            for q in range(G):
                act.wait_ge(cwT_ready, q + 1)
                nc.scalar.activation(g.cwT[0:E, q * CH:(q + 1) * CH], lgT[q % 2][:], ACT.Copy).then_inc(cwh_ready, 1)

        @block.tensor
        def _(pe):
            give(pe, xT_ready)
            if wg is not None:
                pe.wait_ge(wg_split, 2)
            with pe.Fori(0, G // 2) as i:
                for s in range(2):
                    pe.wait_ge(xn_ready, i * 2 + (s + 1))
                    pe.wait_ge(lo_ready, i * 2 + 1)
                    for j in range(GT):
                        last = nc.tensor.transpose(xT[s][:, j * P:(j + 1) * P], xn[s][:, j, :], g.ident[:])
                    last.then_inc(xT_ready, 1)
                if wg is not None:
                    for s in range(2):
                        at = bass.ds(i * (2 * CH) + s * CH, CH)
                        pe.wait_ge(lo_ready, i * 2 + (s + 1) + 1)
                        nc.tensor.matmul(lgT[s][:], wgh[:], g.xh[:, at], start=True, stop=False)
                        nc.tensor.matmul(lgT[s][:], wgl[:], g.xh[:, at], start=False, stop=False)
                        nc.tensor.matmul(lgT[s][:], wgh[:], g.xl[:, at], start=False, stop=True).then_inc(lgT_ready, 1)
                    for s in range(2):
                        pe.wait_ge(wg_split, 2)
                        pe.wait_ge(lgT_copied, i * 2 + (s + 1))
                        pe.wait_ge(lg_copied, i * 2 + 1)
                        for j in range(GT):
                            last = nc.tensor.transpose(lg[s][:, j * E:(j + 1) * E],
                                                       lgT_sb[s][:, j * P:(j + 1) * P], g.ident[0:E, 0:E])
                        last.then_inc(lg_ready, 1)
            if wg is None:
                return
            pe.wait_ge(cw_ready, 1)
            for q in range(G):
                if q >= 2:
                    pe.wait_ge(cwl_ready, q - 1)
                for j in range(GT):
                    last = nc.tensor.transpose(lgT[q % 2][:, j * P:(j + 1) * P], work[2][:, q * GT + j, :], g.ident[:])
                last.then_inc(cwT_ready, 1)


def moe(nc, g, w1, b1, w2, b2, ws1, bs1, ws2, bs2):
    with ExitStack() as st:
        c = Ctx(nc, st)
        c.n = g.stage
        NE, D, F = w1.shape
        FB = F // P
        N = NE + 1
        T = g.resid.shape[1]
        GT = CH // P
        G = T // GT
        NRAW = 2
        w1h, w1l = (c.sb(x, [P, N, F], F32R) for x in ("w1h", "w1l"))
        w2h, w2l = (c.sb(x, [P, N, FB, D], F32R) for x in ("w2h", "w2l"))
        raw = [c.sb(f"raw{s}", [P, F + FB * D]) for s in range(NRAW)]
        b1s = c.sb("b1s", [P, N, FB])
        b2s = c.sb("b2s", [P, N])
        act_f = [c.sb(f"act_f{f}", [P, CH]) for f in range(FB)]
        act_h = [[c.sb(f"act_h{s}{f}", [P, CH], F32R) for f in range(FB)] for s in range(2)]
        act_l = [[c.sb(f"act_l{s}{f}", [P, CH], F32R) for f in range(FB)] for s in range(2)]
        cwb = c.sb("cwb", [P, CH])
        yw = [c.sb(f"yw{s}", [P, CH]) for s in range(2)]
        acc = c.sb("acc", [P, CH])
        hp = [c.ps(f"hp{f}", [P, CH]) for f in range(FB)]
        yp = [c.ps(f"yp{s}", [P, CH]) for s in range(2)]
        cp = c.ps("cp", [P, CH])
        tp = c.ps("tp", [P, GT, P])
        raw_loaded = [c.sem(f"raw_l{s}") for s in range(NRAW)]
        names = ("bias_l", "w_hi", "w_split", "h_r", "hi_r", "silu_r", "lo_r", "y_r", "cp_r", "cwb_r", "yw_r",
                 "acc_r", "tp_r", "res_r")
        (bias_loaded, w_hi, w_split, h_ready, hi_ready, silu_ready, lo_ready, y_ready, cp_ready, cwb_ready,
         yw_ready, acc_ready, tp_ready, resid_ready) = (c.sem(x) for x in names)
        block = st.enter_context(nc.Block())

        @block.sync
        def _(sp):
            with nc.allow_non_contiguous_dma(reason="biases, a few KB"):
                sp.dma_start(b1s[:, 0:NE, :], b1.rearrange("e (f p) -> p e f", p=P)).then_inc(bias_loaded, 16)
                sp.dma_start(b1s[:, NE, :], bs1.rearrange("(f p) -> p f", p=P)).then_inc(bias_loaded, 16)
                sp.dma_start(b2s[:, 0:NE], b2.rearrange("e d -> d e")).then_inc(bias_loaded, 16)
                sp.dma_start(b2s[:, NE:N], bs2.rearrange("(d o) -> d o", o=1)).then_inc(bias_loaded, 16)
            for e in range(N):
                if e >= NRAW:
                    sp.wait_ge(w_split, e - NRAW + 1)
                s = e % NRAW
                up, down = (w1[e], w2[e]) if e < NE else (ws1, ws2)
                sp.dma_start(raw[s][:, 0:F], up).then_inc(raw_loaded[s], 16)
                sp.dma_start(raw[s][:, F:].rearrange("p (f d) -> p f d", f=FB),
                             down.rearrange("(f p) d -> p f d", p=P)).then_inc(raw_loaded[s], 16)

        @block.gpsimd
        def _(pool):
            give(pool, acc_ready)
            with pool.Fori(0, G) as t:
                for e in range(N):
                    pool.wait_ge(yw_ready, t * N + (e + 1) + 1)
                    if e == 0:
                        pool.wait_ge(tp_ready, t + 1)
                        pool_copy(nc, g, acc[:], yw[0][:]).then_inc(acc_ready, 1)
                    else:
                        pool.wait_ge(acc_ready, t * N + e + 1)
                        nc.gpsimd.tensor_tensor(acc[:], acc[:], yw[e % 2][:], ALU.add).then_inc(acc_ready, 1)

        @block.vector
        def _(dve):
            give(dve, lo_ready, cwb_ready, yw_ready, resid_ready)
            for e in range(N):
                s = e % NRAW
                dve.wait_ge(raw_loaded[s], 32 * (e // NRAW + 1))
                up, down = raw[s][:, 0:F], raw[s][:, F:].rearrange("p (f d) -> p f d", f=FB)
                nc.vector.tensor_copy(w1h[:, e], up)
                nc.vector.tensor_copy(w2h[:, e], down).then_inc(w_hi, 1)
                dve.wait_ge(w_hi, e + 1)
                nc.vector.tensor_tensor(w1l[:, e], up, f32(w1h[:, e]), ALU.subtract)
                nc.vector.tensor_tensor(w2l[:, e], down, f32(w2h[:, e]), ALU.subtract).then_inc(w_split, 1)
            dve.wait_ge(bias_loaded, 64)
            with dve.Fori(0, G) as t:
                def weigh(e):
                    dve.wait_ge(y_ready, t * N + (e + 1) + 1)
                    s = e % 2
                    if e >= 2:
                        dve.wait_ge(acc_ready, t * N + (e - 1) + 1)
                    else:
                        dve.wait_ge(acc_ready, t * N + 1)
                    if e < NE:
                        dve.wait_ge(cwb_ready, t * NE + (e + 1) + 1)
                        nc.vector.scalar_tensor_tensor(yw[s][:], yp[s][:], b2s[:, e:e + 1], cwb[:], ALU.add,
                                                       ALU.mult).then_inc(yw_ready, 1)
                    else:
                        nc.vector.tensor_scalar(yw[s][:], yp[s][:], b2s[:, e:e + 1], HALF * SHARED_SCALE, ALU.add,
                                                ALU.mult).then_inc(yw_ready, 1)

                for e in range(N):
                    s = e % 2
                    for f in range(FB):
                        dve.wait_ge(silu_ready, t * (N * FB) + (e * FB + f + 1) + 1)
                        nc.vector.tensor_tensor(act_l[s][f][:], act_f[f][:], f32(act_h[s][f][:]),
                                                ALU.subtract).then_inc(lo_ready, 1)
                    if e >= 1:
                        weigh(e - 1)
                    if e < NE:
                        dve.wait_ge(cp_ready, t * NE + (e + 1))
                        dve.wait_ge(yw_ready, t * N + e + 1)
                        nc.vector.tensor_copy(cwb[:], cp[:]).then_inc(cwb_ready, 1)
                weigh(N - 1)
                dve.wait_ge(tp_ready, t + 1 + 1)
                at = bass.ds(t * GT, GT)
                nc.vector.tensor_tensor(g.resid[:, at, :], tp[:], g.resid[:, at, :], ALU.add).then_inc(resid_ready, 1)

        @block.scalar
        def _(act):
            give(act, silu_ready)
            act.wait_ge(bias_loaded, 64)
            with act.Fori(0, G) as t:
                for e in range(N):
                    s = e % 2
                    for f in range(FB):
                        act.wait_ge(h_ready, t * (N * FB) + (e * FB + f + 1))
                        if e >= 2:
                            act.wait_ge(y_ready, t * N + (e - 1) + 1)
                        else:
                            act.wait_ge(y_ready, t * N + 1)
                        if e >= 1:
                            act.wait_ge(lo_ready, t * (N * FB) + ((e - 1) * FB + f + 1) + 1)
                        else:
                            act.wait_ge(lo_ready, t * (N * FB) + 1)
                        bias = b1s[:, e, f:f + 1]
                        nc.scalar.activation(act_h[s][f][:], hp[f][:], ACT.Silu, bias=bias).then_inc(hi_ready, 1)
                        nc.scalar.activation(act_f[f][:], hp[f][:], ACT.Silu, bias=bias).then_inc(silu_ready, 1)

        @block.tensor
        def _(pe):
            give(pe, y_ready, tp_ready)
            pe.wait_ge(w_split, N)
            with pe.Fori(0, G) as t:
                at = bass.ds(t * CH, CH)

                def up(e):
                    for f in range(FB):
                        if e >= 1:
                            pe.wait_ge(silu_ready, t * (N * FB) + ((e - 1) * FB + f + 1) + 1)
                        else:
                            pe.wait_ge(silu_ready, t * (N * FB) + 1)
                        cols = slice(f * P, (f + 1) * P)
                        nc.tensor.matmul(hp[f][:], w1h[:, e, cols], g.xh[:, at], start=True, stop=False)
                        nc.tensor.matmul(hp[f][:], w1h[:, e, cols], g.xl[:, at], start=False, stop=False)
                        nc.tensor.matmul(hp[f][:], w1l[:, e, cols], g.xh[:, at], start=False, stop=True).then_inc(h_ready, 1)
                    if e < NE:
                        pe.wait_ge(cwb_ready, t * NE + e + 1)
                        nc.tensor.matmul(cp[:], g.select[:, e, :], g.cwT[:, at], start=True, stop=True).then_inc(cp_ready, 1)

                def down(e):
                    s = e % 2
                    if e >= 2:
                        pe.wait_ge(yw_ready, t * N + (e - 1) + 1)
                    else:
                        pe.wait_ge(yw_ready, t * N + 1)
                    for f in range(FB):
                        pe.wait_ge(lo_ready, t * (N * FB) + (e * FB + f + 1) + 1)
                        nc.tensor.matmul(yp[s][:], w2h[:, e, f], act_h[s][f][:], start=f == 0, stop=False)
                        nc.tensor.matmul(yp[s][:], w2l[:, e, f], act_h[s][f][:], start=False, stop=False)
                        last = nc.tensor.matmul(yp[s][:], w2h[:, e, f], act_l[s][f][:], start=False, stop=f == FB - 1)
                    last.then_inc(y_ready, 1)

                for e in range(N):
                    up(e)
                    if e >= 1:
                        down(e - 1)
                down(N - 1)
                pe.wait_ge(acc_ready, t * N + N + 1)
                pe.wait_ge(resid_ready, t + 1)
                for j in range(GT):
                    last = nc.tensor.transpose(tp[:, j, :], acc[:, j * P:(j + 1) * P], g.ident[:])
                last.then_inc(tp_ready, 1)


def attention(nc, g, wq, wk, wv, wo, bo, S):
    with ExitStack() as st:
        c = Ctx(nc, st)
        c.n = g.stage
        D, H, C = wq.shape
        T = g.resid.shape[1]
        B = T * P // S
        NP = H // 2
        ST = S // P
        NC = S // CH
        QT = CH // P
        SCALE = float(C) ** -0.5
        WC = NP * P // CH

        wvh, wvl = (c.sb(x, [P, NP * P], F32R) for x in ("wvh", "wvl"))
        wo_sb = c.sb("wo_sb", [P, NP, D])
        bo_sb = c.sb("bo_sb", [P, 1])
        wraw = c.sb("wraw", [P, 2, P])
        wh, wl = ([c.sb(f"{x}{s}", [P, 2, 2, 2, C], F32R) for s in range(2)] for x in ("wh", "wl"))
        K1, K2, Q1, Q2 = ([[c.sb(f"{x}{s}{a}", [P, S], F32R) for a in range(2)] for s in range(2)]
                          for x in ("K1", "K2", "Q1", "Q2"))
        xbh, xbl = (c.sb(x, [P, S], F32R) for x in ("xbh", "xbl"))
        VZ = c.sb("VZ", [P, NP, S])
        Vs = [c.sb(f"Vs{s}", [P, ST, P]) for s in range(2)]
        Pr = [c.sb(f"Pr{s}", [P, 2, CH]) for s in range(3)]
        nmax2 = [c.sb(f"nmax2{a}", [P, 2, ST]) for a in range(2)]
        nmax = [c.sb(f"nmax{a}", [P, ST]) for a in range(2)]
        diag = [c.sb(f"diag{k}", [P, QT, P], F32R) for k in range(NC)]
        row64 = c.sb("row64", [P, P], F32R)
        zinv = c.sb("zinv", [P, CH])
        oT = [Pr[k][:, 0, :] for k in range(NC)]

        sc = [c.ps(f"sc{s}", [P, 2, CH]) for s in range(2)]
        ring = [c.ps(f"ring{s}", [P, CH]) for s in range(2)]
        zp = c.ps("zp", [P, CH])
        sp_ = c.ps("sp", [P, CH])

        names = ("wv_l", "w_l", "w_s", "wv_s", "pc", "w_free", "ring_r", "ring_f", "hi_r", "lo_r", "k2_r",
                 "nm_r", "nmc_r", "diag_r", "m_r", "st_r", "p_r", "pv_r", "zi_r", "z_r", "xb_r", "v_r", "ve_r", "vc_r",
                 "o_r", "ob_r", "ot_r", "res_r", "set_r")
        (wv_loaded, w_loaded, w_split, wv_split, pool_chain, w_free, ring_ready, ring_free, hi_ready, lo_ready,
         k2_ready, nm_ready, nmc_ready, diag_ready, max_ready, sc_ready, p_ready, pv_ready, zinv_ready, z_ready,
         xb_ready, v_ready, v_copied, vs_ready, o_ready, ob_ready, ot_ready, resid_ready, set_ready) = (
            c.sem(x) for x in names)

        proj = [("proj", a, m, k) for a in range(2) for m in range(2) for k in range(NC)]
        spans = []
        for t in range(ST):
            for half in range(-(-P * (t + 1) // CH)):
                spans.append((t, half, min(CH, P * (t + 1) - CH * half)))
        maxes = [[("max", a, *x) for x in spans] for a in range(2)]
        rows = [[("row", a, k) for k in range(NC)] for a in range(2)]
        jobs = proj + maxes[0] + maxes[1][:4] + rows[0] + maxes[1][4:] + rows[1]
        NJ = len(jobs)
        assert NJ % 2 == 0
        steps = [(k, kt) for k in range(NC)[::-1] for kt in range(QT * (k + 1))]
        NS = len(steps)
        assert NS % 2 == 0 and NS % 3 == 0
        per = [NJ * s // (NS - 1) for s in range(NS)] + [NJ]
        per[NS - 1] = NJ
        NPROJ, NMAX, NROW = len(proj), len(spans) * 2, len(rows) * NC

        def begins(k, kt):
            q0 = max(CH * k, P * kt)
            return q0, CH * (k + 1) - q0

        block = st.enter_context(nc.Block())

        @block.sync
        def _(sp):
            sp.dma_start(VZ[:, 0:NP * P // S, :].rearrange("p a b -> p (a b)"),
                         wv.rearrange("d h c -> d (h c)")).then_inc(wv_loaded, 16)
            for a in range(2):
                sp.dma_start(wo_sb[a * C:(a + 1) * C, :, :],
                             wo.rearrange("c (p two) d -> two c p d", two=2)[a]).then_inc(wv_loaded, 16)
            with nc.allow_non_contiguous_dma(reason="a bias, 512 bytes"):
                sp.dma_start(bo_sb[:], bo.rearrange("(d o) -> d o", o=1)).then_inc(wv_loaded, 16)

            def load(pair):
                for m, w in enumerate((wk, wq)):
                    sp.dma_start(wraw[:, m, :], w.rearrange("d (p h) c -> d p (h c)", h=2)[:, pair, :]).then_inc(w_loaded, 16)

            load(0)
            with sp.Fori(0, B * NP) as u:
                sp.wait_ge(w_free, u + 1)
                n = (u + 1) % NP
                wkq = [w.rearrange("d (p h) c -> d p (h c)", h=2) for w in (wk, wq)]
                for m in range(2):
                    sp.dma_start(wraw[:, m, :], wkq[m][:, bass.ds(n, 1), :]).then_inc(w_loaded, 16)
            sp.wait_ge(w_loaded, 32 * (B * NP + 1))

        @block.gpsimd
        def _(pool):
            give(pool, vs_ready)
            def split(u1, s, first=False):
                pool.wait_ge(w_loaded, u1 * 32 + 32)
                if not first:
                    pool.wait_ge(k2_ready, u1 * (2 * NC))
                for a in range(2):
                    for m in range(2):
                        src = wraw[:, m, a * C:(a + 1) * C].unsqueeze(1).to_broadcast([P, 2, C])
                        pool_copy(nc, g, wh[s][:, a, m], src).then_inc(pool_chain, 1)
                pool.wait_ge(pool_chain, u1 * 4 + 4)
                for a in range(2):
                    for m in range(2):
                        src = wraw[:, m, a * C:(a + 1) * C].unsqueeze(1).to_broadcast([P, 2, C])
                        last = nc.gpsimd.tensor_tensor(wl[s][:, a, m], src, f32(wh[s][:, a, m]), ALU.subtract)
                        if (a, m) == (1, 1):
                            last.then_inc(w_free, 1)

            def keys(u1, s):
                pool.wait_ge(w_free, u1 + 1)
                for a in range(2):
                    for k in range(NC):
                        pool.wait_ge(hi_ready, u1 * NPROJ + (a * 2 * NC + k + 1))
                        at = slice(k * CH, (k + 1) * CH)
                        pool_copy(nc, g, K2[s][a][0:C, at], f32(K1[s][a][0:C, at])).then_inc(k2_ready, 1)

            split(0, 0, first=True)
            keys(0, 0)
            with pool.Fori(0, B) as b:
                pool.wait_ge(v_copied, b * (ST * WC) + ST * WC)
                pool.wait_ge(k2_ready, b * (NP * 2 * NC) + 2 * NC)
                pool_copy(nc, g, Vs[0][:].rearrange("p t c -> p (t c)"), VZ[:, 0, :]).then_inc(vs_ready, 1)
                with pool.Fori(0, NP // 2) as ppq:
                    pp = ppq * 2
                    for j in range(2):
                        u = b * NP + pp + j
                        pool.wait_ge(pv_ready, u * NS + 2 + 1)
                        split(u + 1, 1 - j)
                        if j == 0:
                            nxt = pp + 1
                        else:
                            nxt = (pp + 2) % NP
                            pool.wait_ge(z_ready, u * NC + 1)
                        pool_copy(nc, g, Vs[1 - j][:].rearrange("p t c -> p (t c)"),
                                              VZ[:, bass.ds(nxt, 1), :].rearrange("p a c -> p (a c)")).then_inc(vs_ready, 1)
                        pool.wait_ge(vs_ready, b * (NP + 1) + pp + (j + 2) + 1)
                        keys(u + 1, 1 - j)

        def vs_count(b, pair):
            return b * (NP + 1) + pair + 1

        @block.vector
        def _(dve):
            give(dve, z_ready, resid_ready)
            nc.vector.memset(f32(row64[:]), 0.0).then_inc(set_ready, 1)
            dve.wait_ge(set_ready, 1)
            nc.vector.memset(f32(row64[:, C:C + 1]), 1.0)
            for s in range(2):
                for a in range(2):
                    nc.vector.memset(f32(K2[s][a][C:P, :]), 1.0)
            nc.vector.memset(nmax2[0][:], 3e38)
            nc.vector.memset(nmax2[1][:], 3e38).then_inc(set_ready, 1)
            dve.wait_ge(wv_loaded, 64)
            raw_v = VZ[:, 0:NP * P // S, :].rearrange("p a b -> p (a b)")
            nc.vector.tensor_copy(wvh[:], raw_v).then_inc(wv_split, 1)
            dve.wait_ge(wv_split, 1)
            nc.vector.tensor_tensor(wvl[:], raw_v, f32(wvh[:]), ALU.subtract).then_inc(wv_split, 1)
            dve.wait_ge(set_ready, 2)

            def job(u1, s, n):
                what, a = jobs[n][:2]
                dve.wait_ge(ring_ready, u1 * NJ + (n + 1))
                bank = ring[n % 2]
                if what == "proj":
                    m, k = jobs[n][2:]
                    at = slice(k * CH, (k + 1) * CH)
                    dve.wait_ge(hi_ready, u1 * NPROJ + (n + 1))
                    if m == 0:
                        nc.vector.tensor_tensor(K1[s][a][C:P, at], bank[C:P, :], f32(K1[s][a][C:P, at]),
                                                ALU.subtract).then_inc(ring_free, 1)
                    else:
                        nc.vector.tensor_tensor(Q2[s][a][0:C, at], bank[0:C, :], f32(Q1[s][a][0:C, at]),
                                                ALU.subtract).then_inc(ring_free, 1)
                elif what == "max":
                    t, half, w = jobs[n][2:]
                    nc.vector.tensor_reduce(nmax2[a][:, half, t:t + 1], bank[:, 0:w], AX_X, ALU.max,
                                            negate=True).then_inc(ring_free, 1)
                    if (t, half) == spans[-1][:2]:
                        dve.wait_ge(ring_free, u1 * NJ + (n + 1))
                        nc.vector.tensor_tensor(nmax[a][:], nmax2[a][:, 0, :], nmax2[a][:, 1, :], ALU.min).then_inc(nmc_ready, 1)
                        dve.wait_ge(nmc_ready, u1 * 2 + (a + 1))
                        for k in range(NC):
                            nc.vector.tensor_tensor(
                                diag[k][:], g.ident[:].unsqueeze(1).to_broadcast([P, QT, P]),
                                nmax[a][:, k * QT:(k + 1) * QT].unsqueeze(2).to_broadcast([P, QT, P]),
                                ALU.mult).then_inc(diag_ready, 1)
                else:
                    k = jobs[n][2]
                    nc.vector.tensor_copy(Q2[s][a][C:P, k * CH:(k + 1) * CH], bank[C:P, :]).then_inc(ring_free, 1)

            for n in range(NJ):
                job(0, 0, n)
            with dve.Fori(0, B) as b:
                dve.wait_ge(v_ready, b * (ST * WC) + 1)
                nc.vector.tensor_copy(xbh[:], f32(g.xh[:, bass.ds(b * S, S)]))
                nc.vector.tensor_copy(xbl[:], f32(g.xl[:, bass.ds(b * S, S)])).then_inc(xb_ready, 1)
                with dve.Fori(0, NP // 2) as ppq:
                    pp = ppq * 2
                    for j in range(2):
                        u = b * NP + pp + j

                        def finish(k):
                            i = NC - 1 - k
                            done = sum(1 for x in steps if x[0] >= k)
                            dve.wait_ge(pv_ready, u * NS + (done + 2) + 1)
                            dve.wait_ge(z_ready, u * NC + i + 1)
                            nc.vector.reciprocal(zinv[:], sp_[:]).then_inc(zinv_ready, 1)
                            dve.wait_ge(zinv_ready, u * NC + (i + 1))
                            nc.vector.tensor_tensor(VZ[:, bass.ds(pp + j, 1), k * CH:(k + 1) * CH], zp[:], zinv[:],
                                                    ALU.mult).then_inc(z_ready, 1)

                        for s, (k, kt) in enumerate(steps):
                            if s >= 1 and steps[s - 1][0] != k:
                                finish_at = s + 1
                                pending = steps[s - 1][0]
                            for n in range(per[s], per[s + 1]):
                                job(u + 1, 1 - j, n)
                            if s >= 1 and any(steps[i - 1][0] != steps[i][0] for i in (s,)):
                                finish(steps[s - 1][0])
                        finish(0)
                for k in range(NC):
                    dve.wait_ge(o_ready, b * NC + (k + 1) + 1)
                    nc.vector.tensor_scalar(oT[k], sc[0][:, k, :], bo_sb[:], None, ALU.add).then_inc(ob_ready, 1)
                for k in range(NC):
                    dve.wait_ge(ot_ready, b * NC + (k + 1) + 1)
                    at = bass.ds(b * ST + k * QT, QT)
                    nc.vector.tensor_tensor(g.resid[:, at, :], sc[1][:, k, :].rearrange("p (t d) -> p t d", d=P),
                                            g.resid[:, at, :], ALU.add).then_inc(resid_ready, 1)

        @block.scalar
        def _(act):
            give(act, p_ready, p_ready)

            def job(u1, s, n):
                if jobs[n][0] != "proj":
                    return
                _, a, m, k = jobs[n]
                act.wait_ge(ring_ready, u1 * NJ + (n + 1))
                dst = (K1 if m == 0 else Q1)[s][a]
                nc.scalar.activation(dst[:, k * CH:(k + 1) * CH], ring[n % 2][:], ACT.Copy).then_inc(hi_ready, 1)

            for n in range(NPROJ):
                job(0, 0, n)
            with act.Fori(0, B) as b:
                act.wait_ge(o_ready, b * NC + 1)
                act.wait_ge(vs_ready, b * (NP + 1) + 1)
                act.wait_ge(wv_split, 2)
                for t in range(ST):
                    for w in range(WC):
                        act.wait_ge(v_ready, b * (ST * WC) + (t * WC + w + 1) + 1)
                        n = CH // P
                        nc.scalar.activation(VZ[:, w * n:(w + 1) * n, t * P:(t + 1) * P],
                                             (zp, sp_)[w % 2][:].rearrange("p (a c) -> p a c", c=P),
                                             ACT.Copy).then_inc(v_copied, 1)
                with act.Fori(0, NP // 2) as ppq:
                    pp = ppq * 2
                    for j in range(2):
                        u = b * NP + pp + j
                        for s, (k, kt) in enumerate(steps):
                            act.wait_ge(sc_ready, u * NS + (s + 1))
                            act.wait_ge(pv_ready, u * NS + s + 1)
                            if s == 0:
                                act.wait_ge(ot_ready, b * NC + 1)
                            w = begins(k, kt)[1]
                            nc.scalar.activation(Pr[s % 3][:, :, 0:w], sc[s % 2][:, :, 0:w], ACT.Exp,
                                                 scale=SCALE).then_inc(p_ready, 1)
                            for n in range(per[s], per[s + 1]):
                                job(u + 1, 1 - j, n)

        @block.tensor
        def _(pe):
            mm = nc.tensor.matmul
            give(pe, pv_ready, pv_ready, pv_ready, v_ready, o_ready, ot_ready)
            pe.wait_ge(set_ready, 2)

            def job(u1, s, n, first=False):
                what, a = jobs[n][:2]
                if not (first and n < 2):
                    pe.wait_ge(ring_free, u1 * NJ + (n - 1))
                bank = ring[n % 2]
                if what == "proj":
                    m, k = jobs[n][2:]
                    if n == 0:
                        pe.wait_ge(w_free, u1 + 1)
                    h, l = (w[s][:, a, m].rearrange("p r c -> p (r c)") for w in (wh, wl))
                    at = bass.ds(((u1 // NP) % B) * S + k * CH, CH)
                    mm(bank[:], h, g.xh[:, at], start=True, stop=False)
                    mm(bank[:], h, g.xl[:, at], start=False, stop=False)
                    mm(bank[:], l, g.xh[:, at], start=False, stop=True).then_inc(ring_ready, 1)
                elif what == "max":
                    t, half, w = jobs[n][2:]
                    if t == 0:
                        pe.wait_ge(ring_free, u1 * NJ + 2 * NC * (a + 1))
                    diagonal = CH * half + w == P * (t + 1)
                    last = mm(bank[:, 0:w], Q1[s][a][:, t * P:(t + 1) * P], K1[s][a][:, half * CH:half * CH + w],
                              start=True, stop=not diagonal)
                    if diagonal:
                        last = mm(bank[:, w - P:w], g.ident_b[:], g.mask_keys[:], start=False, stop=True)
                    last.then_inc(ring_ready, 1)
                else:
                    k = jobs[n][2]
                    pe.wait_ge(diag_ready, u1 * NROW + (a * NC + k + 1))
                    mm(bank[:], row64[:], diag[k][:].rearrange("p t q -> p (t q)"), start=True,
                       stop=True).then_inc(ring_ready, 1)

            def scores(u, s_, slot):
                k, kt = steps[s_]
                q0, w = begins(k, kt)
                pe.wait_ge(p_ready, u * NS + s_ + 1)
                if s_ == 0:
                    pe.wait_ge(ring_free, u * NJ + NJ)
                    pe.wait_ge(k2_ready, u * (2 * NC) + 2 * NC)
                for a in range(2):
                    out = sc[s_ % 2][:, a, 0:w]
                    kk = slice(kt * P, (kt + 1) * P)
                    qq = slice(q0, q0 + w)
                    mm(out, K1[slot][a][:, kk], Q1[slot][a][:, qq], start=True, stop=False)
                    if kt >= QT * k:
                        mm(sc[s_ % 2][:, a, 0:P], g.ident_b[:], g.mask_queries[:], start=False, stop=False)
                    last = mm(out, K2[slot][a][:, kk], Q2[slot][a][:, qq], start=False, stop=True)
                last.then_inc(sc_ready, 1)

            def values(u, s_, slot, b, pair):
                k, kt = steps[s_]
                q0, w = begins(k, kt)
                lead = 1
                pe.wait_ge(p_ready, u * NS + (s_ + 1 + lead) + 1)
                if s_ == 0:
                    pe.wait_ge(vs_ready, vs_count(b, pair) + 1)
                if kt == 0:
                    pe.wait_ge(z_ready, u * NC + (NC - 1 - k) + 1)
                first, end = kt == 0, kt == QT * (k + 1) - 1
                for out, left in ((zp, None), (sp_, g.ones[:])):
                    for a in range(2):
                        lhs = Vs[slot][:, kt, a * C:(a + 1) * C] if left is None else left
                        last = mm(out[a * C:(a + 1) * C, q0 - CH * k:CH], lhs, Pr[s_ % 3][:, a, 0:w],
                                  start=first, stop=end)
                last.then_inc(pv_ready, 1)

            for n in range(NJ):
                job(0, 0, n, first=True)
            with pe.Fori(0, B) as b:
                pe.wait_ge(xb_ready, b + 1)
                pe.wait_ge(wv_split, 2)
                for t in range(ST):
                    tt = slice(t * P, (t + 1) * P)
                    for w in range(WC):
                        n = t * WC + w
                        if n >= 2:
                            pe.wait_ge(v_copied, b * (ST * WC) + (n - 1))
                        else:
                            pe.wait_ge(z_ready, b * (NP * NC) + 1)
                        out, cols = (zp, sp_)[w % 2][:], slice(w * CH, (w + 1) * CH)
                        mm(out, xbh[:, tt], wvh[:, cols], start=True, stop=False)
                        mm(out, xbh[:, tt], wvl[:, cols], start=False, stop=False)
                        mm(out, xbl[:, tt], wvh[:, cols], start=False, stop=True).then_inc(v_ready, 1)
                with pe.Fori(0, NP // 2) as ppq:
                    pp = ppq * 2
                    for j in range(2):
                        u = b * NP + pp + j
                        for s in range(NS):
                            scores(u, s, j)
                            for n in range(per[s], per[s + 1]):
                                job(u + 1, 1 - j, n)
                            if s >= 1:
                                values(u, s - 1, j, b, pp + j)
                        values(u, NS - 1, j, b, pp + j)
                pe.wait_ge(z_ready, b * (NP * NC) + NP * NC + 1)
                for k in range(NC):
                    for p in range(NP):
                        last = mm(sc[0][:, k, :], wo_sb[:, p, :], VZ[:, p, k * CH:(k + 1) * CH], start=p == 0,
                                  stop=p == NP - 1)
                    last.then_inc(o_ready, 1)
                for k in range(NC):
                    pe.wait_ge(ob_ready, b * NC + (k + 1))
                    pe.wait_ge(resid_ready, b * NC + 1)
                    for t in range(QT):
                        last = nc.tensor.transpose(sc[1][:, k, t * P:(t + 1) * P], oT[k][:, t * P:(t + 1) * P],
                                                   g.ident[:])
                    last.then_inc(ot_ready, 1)


def store(nc, g, out):
    with ExitStack() as st:
        c = Ctx(nc, st)
        stored = c.sem("stored")
        block = st.enter_context(nc.Block())

        @block.sync
        def _(sp):
            sp.dma_start(out.rearrange("b (t p) d -> p (b t) d", p=P), g.resid[:]).then_inc(stored, 16)
            sp.wait_ge(stored, 16)


def macaron(nc, x, W_Q, W_K, W_V, W_out, b_out, Wg, W1, b1, W2, b2, Ws1, bs1, Ws2, bs2, out, stages=(0, 1, 2)):
    B, S, D = x.shape
    E = Wg.shape[1]
    T = B * S // P
    with ExitStack() as st:
        g = Ctx(nc, st)
        g.n = "g"
        g.resid = g.sb("resid", [P, T, D])
        g.xh, g.xl = g.sb("xh", [P, B * S], F32R), g.sb("xl", [P, B * S], F32R)
        g.ident, g.ident_b = g.sb("ident", [P, P]), g.sb("ident_b", [P, P], BF16)
        g.mask_keys, g.mask_queries = g.sb("mask_keys", [P, P], BF16), g.sb("mask_queries", [P, P], BF16)
        g.ones, g.eps = g.sb("ones", [P, W_Q.shape[2]]), g.sb("eps", [P, 1])
        g.select = g.sb("select", [P, E, P], F32R)
        g.rank_i, g.rank = g.sb("rank_i", [P, E], mybir.dt.int32), g.sb("rank", [P, E])
        g.stage = 0
        load_constants(nc, g, x)
        for layer in stages:
            g.stage = layer
            if layer == 1:
                layernorm(nc, g, None)
                attention(nc, g, W_Q, W_K, W_V, W_out, b_out, S)
            else:
                with nc.sbuf_tensor(f"cwT{layer}", [P, B * S], F32R) as g.cwT:
                    layernorm(nc, g, Wg)
                    moe(nc, g, W1, b1, W2, b2, Ws1, bs1, Ws2, bs2)
        store(nc, g, out)


_INS = ["L0_attn_resid", "L0_attn_W_Q", "L0_attn_W_K", "L0_attn_W_V", "L0_attn_W_out", "L0_attn_b_out", "L0_ffn_Wg",
        "L0_ffn_W1", "L0_ffn_b1", "L0_ffn_W2", "L0_ffn_b2", "L0_ffn_Ws1", "L0_ffn_bs1", "L0_ffn_Ws2", "L0_ffn_bs2"]


def kernel(**inputs):
    import numpy as _np
    import concourse.bacc as _bacc
    from concourse import mybir as _mybir
    from concourse.bass_utils import run_bass_kernel_spmd as _run

    nc = _bacc.Bacc("TRN2", target_bir_lowering=False, num_devices=1)
    arrays, args = {}, []
    for name in _INS:
        a = _np.ascontiguousarray(inputs[name])
        arrays[f"in_{name}"] = a
        args.append(nc.dram_tensor(f"in_{name}", a.shape, _mybir.dt.from_np(a.dtype), kind="ExternalInput").ap())
    out = nc.dram_tensor("out_x", arrays["in_L0_attn_resid"].shape, _mybir.dt.float32, kind="ExternalOutput").ap()
    macaron(nc, *args, out)
    r = _run(nc, [arrays], core_ids=[0])
    return r.results[0]["out_x"]
```

```python
from contextlib import ExitStack

import concourse.bass as bass
from concourse import mybir

F32 = mybir.dt.float32
F32R = mybir.dt.float32r
BF16 = mybir.dt.bfloat16
ALU = mybir.AluOpType
ACT = mybir.ActivationFunctionType
AX_X = mybir.AxisListType.X

P = 128
LO = 32
CH = 512
LN_EPS = 1e-5
TOPK_EPS = 1e-9
SHARED_SCALE = 0.1
HALF = 0.5
NEG = -1e30


def f32(ap):
    return ap.bitcast(F32)


def pool_copy(nc, g, out, in_, p0=0):
    shape = list(in_.shape)
    one = g.ones[p0:p0 + shape[0], 0:1]
    for k in range(len(shape) - 2):
        one = one.unsqueeze(1)
    return nc.gpsimd.tensor_tensor(out, in_, one.to_broadcast(shape), ALU.mult)


def give(eng, *sems):
    for sem in sems:
        eng.sem_inc(sem, 1)


class Ctx:

    def __init__(self, nc, stack):
        self.nc, self.stack, self.n = nc, stack, 0

    def sb(self, name, shape, dt=F32):
        return self.stack.enter_context(self.nc.sbuf_tensor(f"{name}_{self.n}", shape, dt))

    def ps(self, name, shape, dt=F32):
        return self.stack.enter_context(self.nc.psum_tensor(f"{name}_{self.n}", shape, dt))

    def sem(self, name):
        return self.stack.enter_context(self.nc.semaphore(f"{name}_{self.n}"))


def load_constants(nc, g, x):
    with ExitStack() as st:
        c = Ctx(nc, st)
        loaded, zeroed, made = c.sem("c_loaded"), c.sem("c_zeroed"), c.sem("c_made")
        block = st.enter_context(nc.Block())
        T = g.resid.shape[1]

        @block.sync
        def _(sp):
            sp.dma_start(g.resid[:], x.rearrange("b (t p) d -> p (b t) d", p=P)).then_inc(loaded, 16)
            sp.wait_ge(loaded, 16)

        @block.vector
        def _(dve):
            nc.vector.memset(g.ident[:], 0.0)
            nc.vector.memset(g.ident_b[:], 0.0)
            nc.vector.memset(g.mask_keys[:], 0.0)
            nc.vector.memset(g.mask_queries[:], 0.0)
            nc.vector.memset(g.ones[:], 1.0)
            nc.vector.memset(g.eps[:], LN_EPS).then_inc(zeroed, 1)

        @block.gpsimd
        def _(pool):
            pool.wait_ge(zeroed, 1)
            diag = dict(compare_op=ALU.not_equal, fill=1.0, base=0, pattern=[[-1, P]], channel_multiplier=1)
            nc.gpsimd.affine_select(out=g.ident[:], in_=g.ident[:], **diag)
            nc.gpsimd.affine_select(out=g.ident_b[:], in_=g.ident_b[:], **diag)
            nc.gpsimd.affine_select(out=g.mask_keys[:], in_=g.mask_keys[:], compare_op=ALU.is_ge, fill=NEG,
                                    base=0, pattern=[[-1, P]], channel_multiplier=1)
            nc.gpsimd.affine_select(out=g.mask_queries[:], in_=g.mask_queries[:], compare_op=ALU.is_ge,
                                    fill=NEG, base=0, pattern=[[1, P]], channel_multiplier=-1)
            E = g.rank.shape[1]
            nc.gpsimd.iota(g.rank_i[:], pattern=[[-1, E]], base=E, channel_multiplier=0).then_inc(made, 1)
            pool.wait_ge(made, 1)
            nc.gpsimd.tensor_copy(g.rank[:], g.rank_i[:]).then_inc(made, 1)


class ExpertWeights:

    def __init__(self, c, w1, b1, w2, b2, ws1, bs1, ws2, bs2):
        self.dram = w1, b1, w2, b2, ws1, bs1, ws2, bs2
        self.NE, self.D, self.F = NE, D, F = w1.shape
        self.FB = FB = F // P
        self.N = N = NE + 1
        self.up_hi, self.up_lo = (c.sb(x, [P, N, F], F32R) for x in ("up_hi", "up_lo"))
        self.down_hi, self.down_lo = (c.sb(x, [P, N, FB * D], F32R) for x in ("down_hi", "down_lo"))
        self.b1, self.b2 = c.sb("b1s", [P, N, FB]), c.sb("b2s", [P, N])
        self.loaded = [c.sem(f"w_loaded{s}") for s in range(2)]
        self.bias_loaded, self.hi_ready, self.lo_ready = (c.sem(x) for x in ("bias_l", "w_hi", "w_lo"))

    def load(self, nc, sp, raw):
        w1, b1, w2, b2, ws1, bs1, ws2, bs2 = self.dram
        NE, N, F = self.NE, self.N, self.F
        with nc.allow_non_contiguous_dma(reason="biases, a few KB"):
            sp.dma_start(self.b1[:, 0:NE, :], b1.rearrange("e (f p) -> p e f", p=P)).then_inc(self.bias_loaded, 16)
            sp.dma_start(self.b1[:, NE, :], bs1.rearrange("(f p) -> p f", p=P)).then_inc(self.bias_loaded, 16)
            sp.dma_start(self.b2[:, 0:NE], b2.rearrange("e d -> d e")).then_inc(self.bias_loaded, 16)
            sp.dma_start(self.b2[:, NE:N], bs2.rearrange("(d o) -> d o", o=1)).then_inc(self.bias_loaded, 16)
        for e in range(N):
            if e >= 2:
                sp.wait_ge(self.lo_ready, e - 1)
            s = e % 2
            up, down = (w1[e], w2[e]) if e < NE else (ws1, ws2)
            sp.dma_start(raw[s][:, 0:F], up).then_inc(self.loaded[s], 16)
            sp.dma_start(raw[s][:, F:].rearrange("p (f d) -> p f d", f=self.FB),
                         down.rearrange("(f p) d -> p f d", p=P)).then_inc(self.loaded[s], 16)
        sp.wait_ge(self.bias_loaded, 64)

    def split(self, nc, g, pool, raw):
        F = self.F
        for e in range(self.N):
            s = e % 2
            pool.wait_ge(self.loaded[s], 32 * (e // 2 + 1))
            up, down = raw[s][:, 0:F], raw[s][:, F:]
            pool_copy(nc, g, self.up_hi[:, e], up)
            pool_copy(nc, g, self.down_hi[:, e], down).then_inc(self.hi_ready, 1)
            pool.wait_ge(self.hi_ready, e + 1)
            nc.gpsimd.tensor_tensor(self.up_lo[:, e], up, f32(self.up_hi[:, e]), ALU.subtract)
            nc.gpsimd.tensor_tensor(self.down_lo[:, e], down, f32(self.down_hi[:, e]),
                                    ALU.subtract).then_inc(self.lo_ready, 1)


def layernorm(nc, g, wg, weights=None):
    with ExitStack() as st:
        c = Ctx(nc, st)
        c.n = g.stage
        T = g.resid.shape[1]
        GT = CH // P
        G = T // GT
        E = g.rank.shape[1]
        stats = c.sb("stats", [P, T, 6])
        moments = c.sb("moments", [P, T, 2])
        std = c.sb("std", [P, T])
        rstd = c.sb("rstd", [P, T])
        xn = [c.sb(f"xn{s}", [P, GT, P]) for s in range(2)]
        xT = [c.ps(f"xT{s}", [P, CH]) for s in range(2)]
        stats_done, moments_done, std_done, rstd_done = (c.sem(x) for x in ("stats", "mom", "std", "rstd"))
        xn_ready, xT_ready, hi_ready, lo_ready = (c.sem(x) for x in ("xn_r", "xT_r", "hi_r", "lo_r"))
        if wg is not None:
            raw = [c.sb(f"raw{s}", [P, weights.F + weights.FB * weights.D]) for s in range(2)]
            wg_raw = c.sb("wg_raw", [P, E])
            wgh = c.sb("wgh", [P, E], F32R)
            wgl = c.sb("wgl", [P, E], F32R)
            lgT_sb = [c.sb(f"lgT_sb{s}", [E, CH]) for s in range(2)]
            lgT = [c.ps(f"lgT{s}", [E, CH]) for s in range(2)]
            lg = [c.ps(f"lg{s}", [P, GT * E]) for s in range(2)]
            logits = c.sb("logits", [P, T, E])
            work = [c.sb(f"work{s}", [P, T, E]) for s in range(6)]
            col = [c.sb(f"col{s}", [P, T]) for s in range(10)]
            wg_loaded, wg_split = c.sem("wg_l"), c.sem("wg_s")
            lgT_ready, lgT_copied, lg_ready, lg_copied = (c.sem(x) for x in ("lgT_r", "lgT_c", "lg_r", "lg_c"))
            chain, z_ready, exp_ready, cw_ready = (c.sem(x) for x in ("chain", "z_r", "exp_r", "cw_r"))
            cwT_ready, cwh_ready, cwl_ready, cw_zeroed, sel_ready = (
                c.sem(x) for x in ("cwT_r", "cwh_r", "cwl_r", "cw_z", "sel_r"))
        block = st.enter_context(nc.Block())

        if wg is not None:
            @block.sync
            def _(sp):
                sp.dma_start(wg_raw[:], wg).then_inc(wg_loaded, 16)
                weights.load(nc, sp, raw)

            @block.gpsimd
            def _(pool):
                pool.wait_ge(sel_ready, 1)
                for k, first in enumerate((0, LO)):
                    nc.gpsimd.affine_select(out=g.select[:], in_=f32(g.select[:]), compare_op=ALU.not_equal,
                                            fill=1.0, base=-first, pattern=[[-1, E], [0, P]],
                                            channel_multiplier=1).then_inc(sel_ready, 1)
                    pool.wait_ge(sel_ready, k + 2)
                weights.split(nc, g, pool, raw)

        @block.vector
        def _(dve):
            give(dve, lo_ready)
            if wg is not None:
                give(dve, lg_copied)
                nc.vector.memset(f32(g.select[:]), 0.0).then_inc(sel_ready, 1)
            with dve.Fori(0, T // 4) as q:
                for j in range(4):
                    t = q * 4
                    nc.vector.bn_stats(stats[:, bass.ds(t + j, 1), :], g.resid[:, bass.ds(t + j, 1), :]).then_inc(stats_done, 1)
            dve.wait_ge(stats_done, T)
            for t in range(T):
                last = nc.vector.bn_aggr(moments[:, t, :], stats[:, t, :])
            last.then_inc(moments_done, 1)
            dve.wait_ge(std_done, 1)
            nc.vector.reciprocal(rstd[:], std[:]).then_inc(rstd_done, 1)
            dve.wait_ge(rstd_done, 1)
            if wg is not None:
                nc.vector.memset(f32(g.cwT[:]), 0.0).then_inc(cw_zeroed, 1)
                dve.wait_ge(wg_loaded, 16)
                nc.vector.tensor_copy(wgh[:], wg_raw[:]).then_inc(wg_split, 1)
                dve.wait_ge(wg_split, 1)
                nc.vector.tensor_tensor(wgl[:], wg_raw[:], f32(wgh[:]), ALU.subtract).then_inc(wg_split, 1)
            with dve.Fori(0, G // 2) as i:
                for s in range(2):
                    dve.wait_ge(xT_ready, i * 2 + 1)
                    for j in range(GT):
                        k = i * (2 * GT) + (s * GT + j)
                        last = nc.vector.tensor_scalar(
                            xn[s][:, j, :], g.resid[:, bass.ds(k, 1), :], moments[:, bass.ds(k, 1), 0:1],
                            rstd[:, bass.ds(k, 1)], ALU.subtract, ALU.mult)
                    last.then_inc(xn_ready, 1)
                for s in range(2):
                    dve.wait_ge(hi_ready, i * 2 + (s + 1))
                    at = bass.ds(i * (2 * CH) + s * CH, CH)
                    nc.vector.tensor_tensor(g.xl[:, at], xT[s][:], f32(g.xh[:, at]), ALU.subtract).then_inc(lo_ready, 1)
                if wg is not None:
                    for s in range(2):
                        dve.wait_ge(lg_ready, i * 2 + (s + 1))
                        nc.vector.tensor_copy(
                            logits[:, bass.ds(i * (2 * GT) + s * GT, GT), :],
                            lg[s][:].rearrange("p (t e) -> p t e", e=E)).then_inc(lg_copied, 1)
            if wg is None:
                return

            n = [0]

            def link(ins):
                n[0] += 1
                ins.then_inc(chain, 1)
                dve.wait_ge(chain, n[0])

            def over(a):
                return a[:].unsqueeze(2).to_broadcast([P, T, E])

            tt, red = nc.vector.tensor_tensor, nc.vector.tensor_reduce
            rank = g.rank[:].unsqueeze(1).to_broadcast([P, T, E])
            z, e, w2, eq, s1, s2 = work
            mx, se, rs, v1, k1, v2, k2, den, rden, _ = col
            dve.wait_ge(lg_copied, G + 1)
            link(red(mx[:], logits[:], AX_X, ALU.max))
            tt(z[:], logits[:], over(mx), ALU.subtract).then_inc(z_ready, 1)
            dve.wait_ge(exp_ready, 1)
            link(red(se[:], e[:], AX_X, ALU.add))
            link(nc.vector.reciprocal(rs[:], se[:]))
            link(tt(z[:], e[:], over(rs), ALU.mult))
            link(red(v1[:], z[:], AX_X, ALU.max))
            link(tt(eq[:], z[:], over(v1), ALU.is_equal))
            link(tt(w2[:], eq[:], rank, ALU.mult))
            link(red(k1[:], w2[:], AX_X, ALU.max))
            link(tt(s1[:], w2[:], over(k1), ALU.is_equal))
            link(nc.vector.scalar_tensor_tensor(eq[:], s1[:], -2.0, z[:], ALU.mult, ALU.add))
            link(red(v2[:], eq[:], AX_X, ALU.max))
            link(tt(w2[:], eq[:], over(v2), ALU.is_equal))
            link(tt(eq[:], w2[:], rank, ALU.mult))
            link(red(k2[:], eq[:], AX_X, ALU.max))
            link(tt(s2[:], eq[:], over(k2), ALU.is_equal))
            link(tt(den[:], v1[:], v2[:], ALU.add))
            link(nc.vector.tensor_scalar(se[:], den[:], TOPK_EPS, None, ALU.add))
            link(nc.vector.reciprocal(rden[:], se[:]))
            link(nc.vector.tensor_scalar(den[:], rden[:], HALF, None, ALU.mult))
            link(tt(w2[:], s1[:], s2[:], ALU.add))
            link(tt(eq[:], w2[:], z[:], ALU.mult))
            tt(w2[:], eq[:], over(den), ALU.mult).then_inc(cw_ready, 1)
            for q in range(G):
                dve.wait_ge(cwh_ready, q + 1)
                at = slice(q * CH, (q + 1) * CH)
                nc.vector.tensor_tensor(g.cwT[LO:LO + E, at], lgT[q % 2][:], f32(g.cwT[0:E, at]), ALU.subtract).then_inc(cwl_ready, 1)

        @block.scalar
        def _(act):
            act.wait_ge(moments_done, 1)
            nc.scalar.activation(std[:], moments[:, :, 1], ACT.Sqrt, bias=g.eps[:]).then_inc(std_done, 1)
            with act.Fori(0, G // 2) as i:
                for s in range(2):
                    act.wait_ge(xT_ready, i * 2 + (s + 1) + 1)
                    nc.scalar.activation(g.xh[:, bass.ds(i * (2 * CH) + s * CH, CH)], xT[s][:], ACT.Copy).then_inc(hi_ready, 1)
                if wg is not None:
                    for s in range(2):
                        act.wait_ge(lgT_ready, i * 2 + (s + 1))
                        nc.scalar.activation(lgT_sb[s][:], lgT[s][:], ACT.Copy).then_inc(lgT_copied, 1)
            if wg is None:
                return
            act.wait_ge(z_ready, 1)
            act.wait_ge(cw_zeroed, 1)
            nc.scalar.activation(work[1][:], work[0][:], ACT.Exp).then_inc(exp_ready, 1)
            for q in range(G):
                act.wait_ge(cwT_ready, q + 1)
                nc.scalar.activation(g.cwT[0:E, q * CH:(q + 1) * CH], lgT[q % 2][:], ACT.Copy).then_inc(cwh_ready, 1)

        @block.tensor
        def _(pe):
            give(pe, xT_ready)
            if wg is not None:
                pe.wait_ge(wg_split, 2)
            with pe.Fori(0, G // 2) as i:
                for s in range(2):
                    pe.wait_ge(xn_ready, i * 2 + (s + 1))
                    pe.wait_ge(lo_ready, i * 2 + 1)
                    for j in range(GT):
                        last = nc.tensor.transpose(xT[s][:, j * P:(j + 1) * P], xn[s][:, j, :], g.ident[:])
                    last.then_inc(xT_ready, 1)
                if wg is not None:
                    for s in range(2):
                        at = bass.ds(i * (2 * CH) + s * CH, CH)
                        pe.wait_ge(lo_ready, i * 2 + (s + 1) + 1)
                        nc.tensor.matmul(lgT[s][:], wgh[:], g.xh[:, at], start=True, stop=False)
                        nc.tensor.matmul(lgT[s][:], wgl[:], g.xh[:, at], start=False, stop=False)
                        nc.tensor.matmul(lgT[s][:], wgh[:], g.xl[:, at], start=False, stop=True).then_inc(lgT_ready, 1)
                    for s in range(2):
                        pe.wait_ge(wg_split, 2)
                        pe.wait_ge(lgT_copied, i * 2 + (s + 1))
                        pe.wait_ge(lg_copied, i * 2 + 1)
                        for j in range(GT):
                            last = nc.tensor.transpose(lg[s][:, j * E:(j + 1) * E],
                                                       lgT_sb[s][:, j * P:(j + 1) * P], g.ident[0:E, 0:E])
                        last.then_inc(lg_ready, 1)
            if wg is None:
                return
            pe.wait_ge(cw_ready, 1)
            for q in range(G):
                if q >= 2:
                    pe.wait_ge(cwl_ready, q - 1)
                for j in range(GT):
                    last = nc.tensor.transpose(lgT[q % 2][:, j * P:(j + 1) * P], work[2][:, q * GT + j, :], g.ident[:])
                last.then_inc(cwT_ready, 1)


def moe(nc, g, weights):
    with ExitStack() as st:
        c = Ctx(nc, st)
        c.n = g.stage
        NE, N, FB = weights.NE, weights.N, weights.FB
        T = g.resid.shape[1]
        GT = CH // P
        G = T // GT
        w1h, w1l, w2h, w2l = weights.up_hi, weights.up_lo, weights.down_hi, weights.down_lo
        b1s, b2s = weights.b1, weights.b2
        act_f = [c.sb(f"act_f{f}", [P, CH]) for f in range(FB)]
        act_h = [[c.sb(f"act_h{s}{f}", [P, CH], F32R) for f in range(FB)] for s in range(2)]
        act_l = [[c.sb(f"act_l{s}{f}", [P, CH], F32R) for f in range(FB)] for s in range(2)]
        cwb = c.sb("cwb", [P, CH])
        yw = [c.sb(f"yw{s}", [P, CH]) for s in range(2)]
        acc = c.sb("acc", [P, CH])
        hp = [c.ps(f"hp{f}", [P, CH]) for f in range(FB)]
        yp = [c.ps(f"yp{s}", [P, CH]) for s in range(2)]
        cp = c.ps("cp", [P, CH])
        tp = c.ps("tp", [P, GT, P])
        names = ("h_r", "silu_r", "lo_r", "y_r", "cp_r", "cwb_r", "yw_r",
                 "acc_r", "tp_r", "res_r")
        (h_ready, silu_ready, lo_ready, y_ready, cp_ready, cwb_ready,
         yw_ready, acc_ready, tp_ready, resid_ready) = (c.sem(x) for x in names)
        block = st.enter_context(nc.Block())

        def after(eng, sem, count):
            if not isinstance(count, int) or count > 0:
                eng.wait_ge(sem, count)

        def tiles(eng, tile):
            tile(0, 0, False)
            if G > 2:
                with eng.Fori(0, (G - 2) // 2) as i:
                    tile(i * 2 + 1, 1, False)
                    tile(i * 2 + 2, 0, False)
            tile(G - 1, 1, True)

        assert N % 2 == 1 and G % 2 == 0

        @block.gpsimd
        def _(pool):
            def tile(t, par, last):
                for e in range(N):
                    n, s = t * N + e, (par + e) % 2
                    pool.wait_ge(yw_ready, n + 1)
                    if e == 0:
                        after(pool, tp_ready, t)
                        pool_copy(nc, g, acc[:], yw[s][:]).then_inc(acc_ready, 1)
                    else:
                        pool.wait_ge(acc_ready, n)
                        nc.gpsimd.tensor_tensor(acc[:], acc[:], yw[s][:], ALU.add).then_inc(acc_ready, 1)

            tiles(pool, tile)

        @block.vector
        def _(dve):
            def low_halves(n, s):
                for f in range(FB):
                    dve.wait_ge(silu_ready, n * FB + (f + 1))
                    nc.vector.tensor_tensor(act_l[s][f][:], act_f[f][:], f32(act_h[s][f][:]),
                                            ALU.subtract).then_inc(lo_ready, 1)

            def combine_weights(n, m):
                dve.wait_ge(cp_ready, m + 1)
                after(dve, yw_ready, n)
                nc.vector.tensor_copy(cwb[:], cp[:]).then_inc(cwb_ready, 1)

            def residual(t):
                dve.wait_ge(tp_ready, t + 1)
                at = bass.ds(t * GT, GT)
                nc.vector.tensor_tensor(g.resid[:, at, :], tp[:], g.resid[:, at, :], ALU.add).then_inc(resid_ready, 1)

            def tile(t, par, last):
                for e in range(N):
                    n, m, s = t * N + e, t * NE + e, (par + e) % 2
                    if e < N - 1 or not last:
                        low_halves(n + 1, 1 - s)
                    if e == 0 and not (isinstance(t, int) and t == 0):
                        residual(t - 1)
                    dve.wait_ge(y_ready, n + 1)
                    after(dve, acc_ready, n - 1)
                    if e < NE:
                        dve.wait_ge(cwb_ready, m + 1)
                        nc.vector.scalar_tensor_tensor(yw[s][:], yp[s][:], b2s[:, e:e + 1], cwb[:], ALU.add,
                                                       ALU.mult).then_inc(yw_ready, 1)
                    else:
                        nc.vector.tensor_scalar(yw[s][:], yp[s][:], b2s[:, e:e + 1], HALF * SHARED_SCALE, ALU.add,
                                                ALU.mult).then_inc(yw_ready, 1)
                    if e < NE - 1:
                        combine_weights(n + 1, m + 1)
                    elif e == N - 1 and not last:
                        combine_weights(n + 1, m)

            low_halves(0, 0)
            combine_weights(0, 0)
            tiles(dve, tile)
            residual(G - 1)

        @block.scalar
        def _(act):
            def tile(t, par, last):
                for e in range(N):
                    n, s = t * N + e, (par + e) % 2
                    for f in range(FB):
                        act.wait_ge(h_ready, n * FB + (f + 1))
                        after(act, y_ready, n - 1)
                        after(act, lo_ready, (n - 1) * FB + (f + 1))
                        bias = b1s[:, e, f:f + 1]
                        nc.scalar.activation(act_h[s][f][:], hp[f][:], ACT.Silu, bias=bias)
                        nc.scalar.activation(act_f[f][:], hp[f][:], ACT.Silu, bias=bias).then_inc(silu_ready, 1)

            tiles(act, tile)

        @block.tensor
        def _(pe):
            def up(t, e):
                n, m, at = t * N + e, t * NE + e, bass.ds(t * CH, CH)
                for f in range(FB):
                    after(pe, silu_ready, (n - 1) * FB + (f + 1))
                    cols = slice(f * P, (f + 1) * P)
                    nc.tensor.matmul(hp[f][:], w1h[:, e, cols], g.xh[:, at], start=True, stop=False)
                    nc.tensor.matmul(hp[f][:], w1h[:, e, cols], g.xl[:, at], start=False, stop=False)
                    nc.tensor.matmul(hp[f][:], w1l[:, e, cols], g.xh[:, at], start=False, stop=True).then_inc(h_ready, 1)
                if e < NE:
                    after(pe, cwb_ready, m)
                    nc.tensor.matmul(cp[:], g.select[:, e, :], g.cwT[:, at], start=True, stop=True).then_inc(cp_ready, 1)

            def down(t, e, s):
                n = t * N + e
                after(pe, yw_ready, n - 1)
                for f in range(FB):
                    rows = slice(f * P, (f + 1) * P)
                    pe.wait_ge(lo_ready, n * FB + (f + 1))
                    nc.tensor.matmul(yp[s][:], w2h[:, e, rows], act_h[s][f][:], start=f == 0, stop=False)
                    nc.tensor.matmul(yp[s][:], w2l[:, e, rows], act_h[s][f][:], start=False, stop=False)
                    last = nc.tensor.matmul(yp[s][:], w2h[:, e, rows], act_l[s][f][:], start=False, stop=f == FB - 1)
                last.then_inc(y_ready, 1)

            def back(t):
                pe.wait_ge(acc_ready, t * N + N)
                after(pe, resid_ready, t)
                for j in range(GT):
                    last = nc.tensor.transpose(tp[:, j, :], acc[:, j * P:(j + 1) * P], g.ident[:])
                last.then_inc(tp_ready, 1)

            def tile(t, par, last):
                for e in range(N):
                    if e < N - 1:
                        up(t, e + 1)
                    elif not last:
                        up(t + 1, 0)
                    if e == 0 and not (isinstance(t, int) and t == 0):
                        back(t - 1)
                    down(t, e, (par + e) % 2)

            up(0, 0)
            tiles(pe, tile)
            back(G - 1)


def attention(nc, g, wq, wk, wv, wo, bo, S):
    with ExitStack() as st:
        c = Ctx(nc, st)
        c.n = g.stage
        D, H, C = wq.shape
        T = g.resid.shape[1]
        B = T * P // S
        NP = H // 2
        ST = S // P
        NC = S // CH
        QT = CH // P
        NPR = 4
        NRING = 3
        SCALE = float(C) ** -0.5
        WC = NP * P // CH

        wvh, wvl = (c.sb(x, [P, NP * P], F32R) for x in ("wvh", "wvl"))
        wo_sb = c.sb("wo_sb", [P, NP, D])
        bo_sb = c.sb("bo_sb", [P, 1])
        wraw = c.sb("wraw", [P, 2, P])
        wh, wl = ([c.sb(f"{x}{s}", [P, 2, 2, 2, C], F32R) for s in range(2)] for x in ("wh", "wl"))
        K1, K2, Q1, Q2 = ([[c.sb(f"{x}{s}{a}", [P, S], F32R) for a in range(2)] for s in range(2)]
                          for x in ("K1", "K2", "Q1", "Q2"))
        xbh, xbl = (Q1[1][a][:] for a in range(2))
        VZ = c.sb("VZ", [P, NP, S])
        Vs = [c.sb(f"Vs{s}", [P, ST, P]) for s in range(2)]
        Pr = [c.sb(f"Pr{s}", [P, 2, CH]) for s in range(NPR)]
        pacc = [c.sb(f"pacc{k}", [P, 2, CH]) for k in range(NC)]
        nmax2 = [c.sb(f"nmax2{a}", [P, 2, ST]) for a in range(2)]
        nmax = [c.sb(f"nmax{a}", [P, ST]) for a in range(2)]
        diag = [c.sb(f"diag{k}", [P, QT, P], F32R) for k in range(NC)]
        row64 = c.sb("row64", [P, P], F32R)
        ssum = [pacc[0][:, 0, :], c.sb("ssum1", [P, CH])[:]]
        zinv = [pacc[0][:, 1, :], c.sb("zinv1", [P, CH])[:]]
        oT = [Pr[NPR - NC + k][:, 0, :] for k in range(NC)]

        sc = [c.ps(f"sc{s}", [P, 2, CH]) for s in range(2)]
        ring = [c.ps(f"ring{s}", [P, CH]) for s in range(NRING)]
        zp = c.ps("zp", [P, CH])
        outT = zp, ring[0]

        names = ("wv_l", "w_l", "w_s", "wv_s", "pc", "w_free", "ring_r", "ring_f", "hi_r", "lo_r", "k2_r",
                 "nm_r", "nmc_r", "diag_r", "m_r", "st_r", "p_r", "pv_r", "zi_r", "z_r", "xb_r", "v_r", "ve_r", "vc_r", "padd1_r", "padd0_r", "ss_r", "nt_r",
                 "o_r", "ob_r", "ot_r", "res_r", "set_r", "z_t")
        (wv_loaded, w_loaded, w_split, wv_split, pool_chain, w_free, ring_ready, ring_free, hi_ready, lo_ready,
         k2_ready, nm_ready, nmc_ready, diag_ready, max_ready, sc_ready, p_ready, pv_ready, zinv_ready, z_ready,
         xb_ready, v_ready, v_copied, vs_ready, padd1_ready, padd0_ready, ssum_ready, newton, o_ready, ob_ready, ot_ready, resid_ready, set_ready, z_taken) = (
            c.sem(x) for x in names)

        ORDER = list(range(NC))[::-1]
        proj = [("proj", a, m, k) for a in range(2) for m in range(2) for k in range(NC)]
        spans = []
        for t in range(ST):
            for half in range(-(-P * (t + 1) // CH)):
                spans.append((t, half, min(CH, P * (t + 1) - CH * half)))
        maxes = [[("max", a, *x) for x in spans] for a in range(2)]
        rows = [[("row", a, k) for k in ORDER] for a in range(2)]
        jobs = proj[:2 * NC]
        for i, x in enumerate(proj[2 * NC:]):
            jobs += [x] + maxes[0][2 * i:2 * i + 2]
        jobs += maxes[0][4 * NC:] + maxes[1][:4] + rows[0] + maxes[1][4:] + rows[1]
        NJ = len(jobs)
        WLOAD, TAIL, REST, EARLY, F1 = 0, 2, 2, 2, 12
        def begins(k, kt):
            q0 = max(CH * k, P * kt)
            return q0, CH * (k + 1) - q0

        steps = [(k, kt) for k in ORDER for kt in range(QT * (k + 1))]
        NS = len(steps)
        N1 = QT * NC
        N0 = NS - N1
        assert NS % 2 == 0 and NS % NPR == 0 and NC == 2 and N0 == NPR
        NEXTS = NJ - REST
        load = [0 if i == 0 else 2 * begins(*steps[i])[1] + 4 * begins(*steps[i - 1])[1] + WLOAD for i in range(NS)]
        per = [min(NEXTS, NEXTS * sum(load[:i]) // sum(load[:NS - TAIL])) for i in range(NS + 1)]
        slots = [[jobs[n] for n in range(per[i], per[i + 1])] for i in range(NS)]
        slots[N1 + 1].append(("sum", 0, 1))
        slots.append(jobs[NEXTS:] + [("sum", 0, 0)])
        flat = [x for slot in slots for x in slot]
        SUM0 = ("sum", 0, 0)
        begin = [sum(len(x) for x in slots[:i]) for i in range(NS + 2)]
        before = [len(x) * EARLY // 4 if i else 0 for i, x in enumerate(slots)]
        NL = len(flat)

        def ring_count(u, n):
            return u * NL + (NJ + n)

        def since(n, looped):
            if n >= NRING:
                return NRING
            if not looped:
                return None
            return next(n + NL - i for i in range(NL)[::-1] if i % NRING == n)

        def first_count(x):
            return jobs.index(x) + 1

        def loop_count(u):
            return lambda x: ring_count(u, flat.index(x) + 1)

        FIN = NS - 1
        NPROJ, NMAX, NROW = len(proj), len(spans) * 2, len(rows) * NC

        block = st.enter_context(nc.Block())

        @block.sync
        def _(sp):
            sp.dma_start(VZ[:, 0:NP * P // S, :].rearrange("p a b -> p (a b)"),
                         wv.rearrange("d h c -> d (h c)")).then_inc(wv_loaded, 16)
            for a in range(2):
                sp.dma_start(wo_sb[a * C:(a + 1) * C, :, :],
                             wo.rearrange("c (p two) d -> two c p d", two=2)[a]).then_inc(wv_loaded, 16)
            with nc.allow_non_contiguous_dma(reason="a bias, 512 bytes"):
                sp.dma_start(bo_sb[:], bo.rearrange("(d o) -> d o", o=1)).then_inc(wv_loaded, 16)

            def load(pair):
                for m, w in enumerate((wk, wq)):
                    sp.dma_start(wraw[:, m, :], w.rearrange("d (p h) c -> d p (h c)", h=2)[:, pair, :]).then_inc(w_loaded, 16)

            load(0)
            with sp.Fori(0, B * NP + 1) as u:
                sp.wait_ge(w_free, u + 1)
                n = (u + 1) % NP
                wkq = [w.rearrange("d (p h) c -> d p (h c)", h=2) for w in (wk, wq)]
                for m in range(2):
                    sp.dma_start(wraw[:, m, :], wkq[m][:, bass.ds(n, 1), :]).then_inc(w_loaded, 16)
            sp.wait_ge(w_loaded, 32 * (B * NP + 2))

        @block.gpsimd
        def _(pool):
            give(pool, vs_ready)
            def split(n, s):
                pool.wait_ge(w_loaded, n * 32 + 32)
                for a in range(2):
                    for m in range(2):
                        src = wraw[:, m, a * C:(a + 1) * C].unsqueeze(1).to_broadcast([P, 2, C])
                        pool_copy(nc, g, wh[s][:, a, m], src).then_inc(pool_chain, 1)
                pool.wait_ge(pool_chain, n * 4 + 4)
                for a in range(2):
                    for m in range(2):
                        src = wraw[:, m, a * C:(a + 1) * C].unsqueeze(1).to_broadcast([P, 2, C])
                        last = nc.gpsimd.tensor_tensor(wl[s][:, a, m], src, f32(wh[s][:, a, m]), ALU.subtract)
                        if (a, m) == (1, 1):
                            last.then_inc(w_free, 1)

            def keys(u1, s, a):
                for k in range(NC):
                    pool.wait_ge(hi_ready, u1 * NPROJ + (a * 2 * NC + k + 1))
                    at = slice(k * CH, (k + 1) * CH)
                    pool_copy(nc, g, K2[s][a][0:C, at], f32(K1[s][a][0:C, at])).then_inc(k2_ready, 1)

            split(0, 0)
            split(1, 1)
            pool.wait_ge(w_free, 2)
            keys(0, 0, 0)
            keys(0, 0, 1)
            with pool.Fori(0, B) as b:
                pool.wait_ge(v_copied, b * (ST * WC) + ST * WC)
                pool.wait_ge(k2_ready, b * (NP * 2 * NC) + 2 * NC)
                pool_copy(nc, g, Vs[0][:].rearrange("p t c -> p (t c)"), VZ[:, 0, :]).then_inc(vs_ready, 1)
                with pool.Fori(0, NP // 2) as ppq:
                    pp = ppq * 2
                    for j in range(2):
                        u = b * NP + pp + j
                        for s, (k, kt) in enumerate(steps):
                            if s < N1:
                                q0, w = begins(k, kt)
                                pool.wait_ge(p_ready, u * NS + (s + 3))
                                new, old = Pr[s % NPR][:, :, 0:w], pacc[k][:, :, CH - w:CH]
                                if kt == 0:
                                    pool.wait_ge(ring_ready, ring_count(u, flat.index(("sum", 0, k)) + 1 - NL))
                                    pool_copy(nc, g, old, new).then_inc(padd1_ready, 1)
                                else:
                                    pool.wait_ge(padd1_ready, u * N1 + s)
                                    nc.gpsimd.tensor_tensor(old, old, new, ALU.add).then_inc(padd1_ready, 1)
                            if s in (3, 5):
                                pool.wait_ge(padd1_ready, u * N1 + (s + 1))
                                keys(u + 1, 1 - j, (s - 3) // 2)
                                pool.wait_ge(k2_ready, u * (2 * NC) + (2 * NC + (s - 1) // 2 * NC))
                            if s == 1:
                                pool.wait_ge(pv_ready, u * NS + NPR)
                                if j == 0:
                                    nxt = pp + 1
                                else:
                                    nxt = (pp + 2) % NP
                                    pool.wait_ge(z_ready, u * NC + 2)
                                pool_copy(nc, g, Vs[1 - j][:].rearrange("p t c -> p (t c)"),
                                          VZ[:, bass.ds(nxt, 1), :].rearrange("p a c -> p (a c)")).then_inc(vs_ready, 1)
                                split(u + 2, j)

        def vs_count(b, pair):
            return b * (NP + 1) + pair + 1

        @block.vector
        def _(dve):
            give(dve, z_ready, z_ready, resid_ready, *[padd0_ready] * NPR)
            nc.vector.memset(f32(row64[:]), 0.0).then_inc(set_ready, 1)
            dve.wait_ge(set_ready, 1)
            nc.vector.memset(f32(row64[:, C:C + 1]), 1.0)
            for s in range(2):
                for a in range(2):
                    nc.vector.memset(f32(K2[s][a][C:P, :]), 1.0)
            nc.vector.memset(nmax2[0][:], 3e38)
            nc.vector.memset(nmax2[1][:], 3e38).then_inc(set_ready, 1)
            dve.wait_ge(wv_loaded, 64)
            raw_v = VZ[:, 0:NP * P // S, :].rearrange("p a b -> p (a b)")
            nc.vector.tensor_copy(wvh[:], raw_v).then_inc(wv_split, 1)
            dve.wait_ge(wv_split, 1)
            nc.vector.tensor_tensor(wvl[:], raw_v, f32(wvh[:]), ALU.subtract).then_inc(wv_split, 1)
            dve.wait_ge(set_ready, 2)

            def job(u1, s, x, count_of):
                what, a = x[:2]
                count = count_of(x)
                dve.wait_ge(ring_ready, count)
                if what == "proj":
                    m, k = x[2:]
                    at = slice(k * CH, (k + 1) * CH)
                    dve.wait_ge(hi_ready, u1 * NPROJ + (proj.index(x) + 1))
                    if m == 0:
                        nc.vector.tensor_tensor(K1[s][a][C:P, at], bank[C:P, :], f32(K1[s][a][C:P, at]),
                                                ALU.subtract).then_inc(ring_free, 1)
                    else:
                        nc.vector.tensor_tensor(Q2[s][a][0:C, at], bank[0:C, :], f32(Q1[s][a][0:C, at]),
                                                ALU.subtract).then_inc(ring_free, 1)
                elif what == "sum":
                    nc.vector.tensor_copy(ssum[x[2]], bank[:]).then_inc(ring_free, 1)
                elif what == "max":
                    t, half, w = x[2:]
                    nc.vector.tensor_reduce(nmax2[a][:, half, t:t + 1], bank[:, 0:w], AX_X, ALU.max,
                                            negate=True).then_inc(ring_free, 1)
                    if (t, half) == spans[-1][:2]:
                        dve.wait_ge(ring_free, count)
                        nc.vector.tensor_tensor(nmax[a][:], nmax2[a][:, 0, :], nmax2[a][:, 1, :], ALU.min).then_inc(nmc_ready, 1)
                        dve.wait_ge(nmc_ready, u1 * 2 + (a + 1))
                        for k in ORDER:
                            nc.vector.tensor_tensor(
                                diag[k][:], g.ident[:].unsqueeze(1).to_broadcast([P, QT, P]),
                                nmax[a][:, k * QT:(k + 1) * QT].unsqueeze(2).to_broadcast([P, QT, P]),
                                ALU.mult).then_inc(diag_ready, 1)
                else:
                    k = x[2]
                    nc.vector.tensor_copy(Q2[s][a][C:P, k * CH:(k + 1) * CH], bank[C:P, :]).then_inc(ring_free, 1)

            for n in range(NJ):
                bank = ring[n % NRING]
                job(0, 0, jobs[n], first_count)
            def batch_x(b):
                nc.vector.tensor_copy(xbh, f32(g.xh[:, bass.ds(b * S, S)]))
                nc.vector.tensor_copy(xbl, f32(g.xl[:, bass.ds(b * S, S)])).then_inc(xb_ready, 1)

            batch_x(0)
            with dve.Fori(0, B) as b:
                with dve.Fori(0, NP // 2) as ppq:
                    pp = ppq * 2
                    for j in range(2):
                        u = b * NP + pp + j

                        def over_sums(k):
                            i = ORDER.index(k)
                            dve.wait_ge(z_taken, u * NC + (i + 2))
                            dve.wait_ge(zinv_ready, u * NC + (i + 1))
                            z = VZ[:, bass.ds(pp + j, 1), k * CH:(k + 1) * CH]
                            nc.vector.tensor_tensor(z, z, zinv[k], ALU.mult)
                            nc.vector.scalar_tensor_tensor(ssum[k], ssum[k], -1.0, zinv[k], ALU.mult,
                                                           ALU.mult).then_inc(newton, 1)

                        def corrected(k):
                            z = VZ[:, bass.ds(pp + j, 1), k * CH:(k + 1) * CH]
                            dve.wait_ge(newton, u * NC + (ORDER.index(k) + 1))
                            nc.vector.scalar_tensor_tensor(z, ssum[k], 2.0, z, ALU.add, ALU.mult).then_inc(z_ready, 1)

                        def add(i):
                            w = begins(*steps[i])[1]
                            new, old = Pr[i % NPR][:, :, 0:w], pacc[0][:, :, CH - w:CH]
                            dve.wait_ge(p_ready, u * NS + (i + 3))
                            if i == N1:
                                nc.vector.tensor_copy(old, new).then_inc(padd0_ready, 1)
                            else:
                                dve.wait_ge(padd0_ready, u * N0 + (i - N1 + NPR))
                                nc.vector.tensor_tensor(old, old, new, ALU.add).then_inc(padd0_ready, 1)

                        for i, slot in enumerate(slots):
                            for n, x in enumerate(slot, begin[i]):
                                if i == NS and x == SUM0:
                                    add(NS - 1)
                                    over_sums(1)
                                bank = ring[n % NRING]
                                job(u + 1, 1 - j, x, loop_count(u))
                            if N1 <= i < NS - 1:
                                add(i)
                        corrected(1)
                        over_sums(0)
                        corrected(0)
                batch_x((b + 1) % B)
                for k in range(NC):
                    dve.wait_ge(o_ready, b * NC + (k + 1) + 1)
                    nc.vector.tensor_scalar(oT[k], sc[1][:, k, :], bo_sb[:], None, ALU.add).then_inc(ob_ready, 1)
                for k in range(NC):
                    dve.wait_ge(ot_ready, b * NC + (k + 1) + 1)
                    at = bass.ds(b * ST + k * QT, QT)
                    nc.vector.tensor_tensor(g.resid[:, at, :], outT[k][:].rearrange("p (t d) -> p t d", d=P),
                                            g.resid[:, at, :], ALU.add).then_inc(resid_ready, 1)

        @block.scalar
        def _(act):
            give(act, p_ready, p_ready, z_taken)
            nc.scalar.preload_act_table_set("natural_log_exp_and_others")

            def job(s, n, x, count):
                _, a, m, k = x
                act.wait_ge(ring_ready, count)
                dst = (K1 if m == 0 else Q1)[s][a]
                nc.scalar.activation(dst[:, k * CH:(k + 1) * CH], ring[n % NRING][:], ACT.Copy).then_inc(hi_ready, 1)

            def exponential(u, s):
                act.wait_ge(sc_ready, u * NS + (s + 1))
                act.wait_ge(pv_ready, u * NS + (s + 1))
                if s < NPR:
                    act.wait_ge(padd0_ready, u * N0 + (s + 1))
                else:
                    act.wait_ge(padd1_ready, u * N1 + (s - NPR + 1))
                w = begins(*steps[s])[1]
                nc.scalar.activation(Pr[s % NPR][:, :, 0:w], sc[s % 2][:, :, 0:w], ACT.Exp,
                                     scale=SCALE).then_inc(p_ready, 1)

            for n, x in enumerate(jobs):
                if x[0] == "proj":
                    job(0, n, x, n + 1)
            exponential(0, 0)
            with act.Fori(0, B) as b:
                act.wait_ge(o_ready, b * NC + 1)
                act.wait_ge(vs_ready, b * (NP + 1) + 1)
                act.wait_ge(wv_split, 2)
                for t in range(ST):
                    for w in range(WC):
                        act.wait_ge(v_ready, b * (ST * WC) + (t * WC + w + 1) + 1)
                        n = CH // P
                        nc.scalar.activation(VZ[:, w * n:(w + 1) * n, t * P:(t + 1) * P],
                                             sc[1][:, w % 2, :].rearrange("p (a c) -> p a c", c=P),
                                             ACT.Copy).then_inc(v_copied, 1)
                with act.Fori(0, NP // 2) as ppq:
                    pp = ppq * 2
                    for j in range(2):
                        u = b * NP + pp + j

                        def take(k):
                            done = sum(1 for x in steps if x[0] >= k)
                            act.wait_ge(pv_ready, u * NS + (done + NPR))
                            nc.scalar.activation(VZ[:, bass.ds(pp + j, 1), k * CH:(k + 1) * CH], zp[:],
                                                 ACT.Copy).then_inc(z_taken, 1)

                        def inverse(k):
                            n = flat.index(("sum", 0, k))
                            act.wait_ge(ring_free, ring_count(u, n + 1))
                            nc.scalar.activation(zinv[k], ssum[k], ACT.Ln).then_inc(ssum_ready, 1)
                            act.wait_ge(ssum_ready, u * NC + (NC - k))
                            nc.scalar.activation(zinv[k], zinv[k], ACT.Exp, scale=-1.0).then_inc(zinv_ready, 1)

                        def projections(first, end):
                            for i in range(first, end):
                                if slots[s][i][0] == "proj":
                                    job(1 - j, begin[s] + i, slots[s][i], ring_count(u, begin[s] + i + 1))

                        for s in range(NS):
                            projections(0, before[s])
                            if s == NPR - NC:
                                act.wait_ge(ot_ready, b * NC + 1)
                            if s:
                                exponential(u, s)
                            if s == N1:
                                take(1)
                            projections(before[s], len(slots[s]))
                            if s == FIN:
                                inverse(1)
                        take(0)
                        exponential(u + 1, 0)
                        inverse(0)

        @block.tensor
        def _(pe):
            mm = nc.tensor.matmul
            give(pe, *[pv_ready] * NPR, v_ready, o_ready, ot_ready)
            pe.wait_ge(set_ready, 2)

            def job(u1, s, n, x, count_of):
                what, a = x[:2]
                count, bank = count_of(x), ring[n % NRING]
                back = since(n, not isinstance(count, int))
                if back:
                    pe.wait_ge(ring_free, count - back)
                if what == "sum":
                    k = x[2]
                    if k == 1:
                        pe.wait_ge(padd1_ready, (u1 - 1) * N1 + N1)
                    else:
                        pe.wait_ge(padd0_ready, (u1 - 1) * N0 + (N0 + NPR))
                    for a in range(2):
                        last = mm(bank[a * C:(a + 1) * C, :], g.ones[:], pacc[k][:, a, :], start=True, stop=True)
                    last.then_inc(ring_ready, 1)
                elif what == "proj":
                    m, k = x[2:]
                    if (a, m, k) == (0, 0, 0):
                        pe.wait_ge(w_free, u1 + 1)
                    h, l = (w[s][:, a, m].rearrange("p r c -> p (r c)") for w in (wh, wl))
                    at = bass.ds(((u1 // NP) % B) * S + k * CH, CH)
                    mm(bank[:], h, g.xh[:, at], start=True, stop=False)
                    mm(bank[:], h, g.xl[:, at], start=False, stop=False)
                    mm(bank[:], l, g.xh[:, at], start=False, stop=True).then_inc(ring_ready, 1)
                elif what == "max":
                    t, half, w = x[2:]
                    if t == 0:
                        pe.wait_ge(ring_free, count_of(("proj", a, 1, NC - 1)))
                    diagonal = CH * half + w == P * (t + 1)
                    last = mm(bank[:, 0:w], Q1[s][a][:, t * P:(t + 1) * P], K1[s][a][:, half * CH:half * CH + w],
                              start=True, stop=not diagonal)
                    if diagonal:
                        last = mm(bank[:, w - P:w], g.ident_b[:], g.mask_keys[:], start=False, stop=True)
                    last.then_inc(ring_ready, 1)
                else:
                    k = x[2]
                    pe.wait_ge(diag_ready, u1 * NROW + (a * NC + ORDER.index(k) + 1))
                    mm(bank[:], row64[:], diag[k][:].rearrange("p t q -> p (t q)"), start=True,
                       stop=True).then_inc(ring_ready, 1)

            def scores(u, s_, slot):
                k, kt = steps[s_]
                q0, w = begins(k, kt)
                pe.wait_ge(p_ready, u * NS + s_ + 1)
                if s_ == 0:
                    pe.wait_ge(ring_free, ring_count(u, 0) - (0 if isinstance(u, int) else 2))
                    pe.wait_ge(k2_ready, u * (2 * NC) + 2 * NC)
                for a in range(2):
                    out = sc[s_ % 2][:, a, 0:w]
                    kk = slice(kt * P, (kt + 1) * P)
                    qq = slice(q0, q0 + w)
                    mm(out, K1[slot][a][:, kk], Q1[slot][a][:, qq], start=True, stop=False)
                    if kt >= QT * k:
                        mm(sc[s_ % 2][:, a, 0:P], g.ident_b[:], g.mask_queries[:], start=False, stop=False)
                    last = mm(out, K2[slot][a][:, kk], Q2[slot][a][:, qq], start=False, stop=True)
                    if a == 1:
                        last.then_inc(sc_ready, 1)
                    yield

            def values(u, s_, slot, b, pair):
                k, kt = steps[s_]
                q0, w = begins(k, kt)
                pe.wait_ge(p_ready, u * NS + (s_ + 3))
                if s_ == 0:
                    pe.wait_ge(vs_ready, vs_count(b, pair) + 1)
                if kt == 0:
                    pe.wait_ge(z_taken, u * NC + (NC - k))
                first, end = kt == 0, kt == QT * (k + 1) - 1
                for a in range(2):
                    last = mm(zp[a * C:(a + 1) * C, q0 - CH * k:CH], Vs[slot][:, kt, a * C:(a + 1) * C],
                              Pr[s_ % NPR][:, a, 0:w], start=first, stop=end)
                    if a == 1:
                        last.then_inc(pv_ready, 1)
                    yield

            for n in range(NJ):
                job(0, 0, n, jobs[n], first_count)
            for _ in scores(0, 0, 0):
                pass
            with pe.Fori(0, B) as b:
                pe.wait_ge(xb_ready, b + 1)
                pe.wait_ge(wv_split, 2)
                for t in range(ST):
                    tt = slice(t * P, (t + 1) * P)
                    for w in range(WC):
                        n = t * WC + w
                        if n >= 2:
                            pe.wait_ge(v_copied, b * (ST * WC) + (n - 1))
                        elif n == 0:
                            pe.wait_ge(resid_ready, b * NC + 1)
                        out, cols = sc[1][:, w % 2, :], slice(w * CH, (w + 1) * CH)
                        mm(out, xbh[:, tt], wvh[:, cols], start=True, stop=False)
                        mm(out, xbh[:, tt], wvl[:, cols], start=False, stop=False)
                        mm(out, xbl[:, tt], wvh[:, cols], start=False, stop=True).then_inc(v_ready, 1)
                with pe.Fori(0, NP // 2) as ppq:
                    pp = ppq * 2
                    for j in range(2):
                        u = b * NP + pp + j
                        for s in range(NS):
                            if (j, s) == (0, 1):
                                pe.wait_ge(v_copied, b * (ST * WC) + ST * WC)
                            parts = [scores(u, s, j)] * 2 if s else []
                            if s >= 1:
                                parts += [values(u, s - 1, j, b, pp + j)] * 2
                            own = list(enumerate(slots[s], begin[s]))
                            if not parts:
                                parts = [iter([None])]
                            for i, part in enumerate(parts):
                                next(part)
                                for n, x in own[len(own) * i // len(parts):len(own) * (i + 1) // len(parts)]:
                                    job(u + 1, 1 - j, n, x, loop_count(u))
                        for n, x in enumerate(slots[NS][:-1], begin[NS]):
                            job(u + 1, 1 - j, n, x, loop_count(u))
                        for _ in values(u, NS - 1, j, b, pp + j):
                            pass
                        for _ in scores(u + 1, 0, 1 - j):
                            pass
                        job(u + 1, 1 - j, NL - 1, SUM0, loop_count(u))
                for done, pairs in ((NP - 1, range(NP - 1)), (NP, (NP - 1,))):
                    pe.wait_ge(z_ready, b * (NP * NC) + (done * NC + 2))
                    for k in range(NC):
                        for p in pairs:
                            last = mm(sc[1][:, k, :], wo_sb[:, p, :], VZ[:, p, k * CH:(k + 1) * CH], start=p == 0,
                                      stop=p == NP - 1)
                        if done == NP:
                            last.then_inc(o_ready, 1)
                for k in range(NC):
                    pe.wait_ge(ob_ready, b * NC + (k + 1))
                    for t in range(QT):
                        last = nc.tensor.transpose(outT[k][:, t * P:(t + 1) * P], oT[k][:, t * P:(t + 1) * P],
                                                   g.ident[:])
                    last.then_inc(ot_ready, 1)


def store(nc, g, out):
    with ExitStack() as st:
        c = Ctx(nc, st)
        stored = c.sem("stored")
        block = st.enter_context(nc.Block())

        @block.sync
        def _(sp):
            sp.dma_start(out.rearrange("b (t p) d -> p (b t) d", p=P), g.resid[:]).then_inc(stored, 16)
            sp.wait_ge(stored, 16)


def macaron(nc, x, W_Q, W_K, W_V, W_out, b_out, Wg, W1, b1, W2, b2, Ws1, bs1, Ws2, bs2, out, stages=(0, 1, 2)):
    B, S, D = x.shape
    E = Wg.shape[1]
    T = B * S // P
    with ExitStack() as st:
        g = Ctx(nc, st)
        g.n = "g"
        g.resid = g.sb("resid", [P, T, D])
        g.xh, g.xl = g.sb("xh", [P, B * S], F32R), g.sb("xl", [P, B * S], F32R)
        g.ident, g.ident_b = g.sb("ident", [P, P]), g.sb("ident_b", [P, P], BF16)
        g.mask_keys, g.mask_queries = g.sb("mask_keys", [P, P], BF16), g.sb("mask_queries", [P, P], BF16)
        g.ones, g.eps = g.sb("ones", [P, W_Q.shape[2]]), g.sb("eps", [P, 1])
        g.rank_i, g.rank = g.sb("rank_i", [P, E], mybir.dt.int32), g.sb("rank", [P, E])
        g.stage = 0
        load_constants(nc, g, x)
        for layer in stages:
            g.stage = layer
            if layer == 1:
                layernorm(nc, g, None)
                attention(nc, g, W_Q, W_K, W_V, W_out, b_out, S)
            else:
                with ExitStack() as inner:
                    c = Ctx(nc, inner)
                    c.n = layer
                    g.cwT, g.select = c.sb("cwT", [P, B * S], F32R), c.sb("select", [P, E, P], F32R)
                    weights = ExpertWeights(c, W1, b1, W2, b2, Ws1, bs1, Ws2, bs2)
                    layernorm(nc, g, Wg, weights)
                    moe(nc, g, weights)
        store(nc, g, out)


_INS = ["L0_attn_resid", "L0_attn_W_Q", "L0_attn_W_K", "L0_attn_W_V", "L0_attn_W_out", "L0_attn_b_out", "L0_ffn_Wg",
        "L0_ffn_W1", "L0_ffn_b1", "L0_ffn_W2", "L0_ffn_b2", "L0_ffn_Ws1", "L0_ffn_bs1", "L0_ffn_Ws2", "L0_ffn_bs2"]


def kernel(**inputs):
    import numpy as _np
    import concourse.bacc as _bacc
    from concourse import mybir as _mybir
    from concourse.bass_utils import run_bass_kernel_spmd as _run

    nc = _bacc.Bacc("TRN2", target_bir_lowering=False, num_devices=1)
    arrays, args = {}, []
    for name in _INS:
        a = _np.ascontiguousarray(inputs[name])
        arrays[f"in_{name}"] = a
        args.append(nc.dram_tensor(f"in_{name}", a.shape, _mybir.dt.from_np(a.dtype), kind="ExternalInput").ap())
    out = nc.dram_tensor("out_x", arrays["in_L0_attn_resid"].shape, _mybir.dt.float32, kind="ExternalOutput").ap()
    macaron(nc, *args, out)
    r = _run(nc, [arrays], core_ids=[0])
    return r.results[0]["out_x"]
```

```python
from contextlib import ExitStack

import concourse.bass as bass
from concourse import mybir

F32 = mybir.dt.float32
F32R = mybir.dt.float32r
BF16 = mybir.dt.bfloat16
ALU = mybir.AluOpType
ACT = mybir.ActivationFunctionType
AX_X = mybir.AxisListType.X

P = 128
LO = 32
CH = 512
LN_EPS = 1e-5
TOPK_EPS = 1e-9
SHARED_SCALE = 0.1
HALF = 0.5
NEG = -1e30


def f32(ap):
    return ap.bitcast(F32)


def pool_copy(nc, g, out, in_, p0=0):
    shape = list(in_.shape)
    one = g.ones[p0:p0 + shape[0], 0:1]
    for k in range(len(shape) - 2):
        one = one.unsqueeze(1)
    return nc.gpsimd.tensor_tensor(out, in_, one.to_broadcast(shape), ALU.mult)


def give(eng, *sems):
    for sem in sems:
        eng.sem_inc(sem, 1)


def row_stats(nc, g, first, tiles):
    for j in range(tiles):
        at = bass.ds(first + j, 1)
        last = nc.vector.bn_stats(g.stats[:, at, :], g.resid[:, at, :])
    return last


class Ctx:

    def __init__(self, nc, stack):
        self.nc, self.stack, self.n = nc, stack, 0

    def sb(self, name, shape, dt=F32):
        return self.stack.enter_context(self.nc.sbuf_tensor(f"{name}_{self.n}", shape, dt))

    def ps(self, name, shape, dt=F32):
        return self.stack.enter_context(self.nc.psum_tensor(f"{name}_{self.n}", shape, dt))

    def sem(self, name):
        return self.stack.enter_context(self.nc.semaphore(f"{name}_{self.n}"))


def load_constants(nc, g, x):
    with ExitStack() as st:
        c = Ctx(nc, st)
        loaded, zeroed, made = c.sem("c_loaded"), c.sem("c_zeroed"), c.sem("c_made")
        block = st.enter_context(nc.Block())
        T = g.resid.shape[1]

        @block.sync
        def _(sp):
            sp.dma_start(g.resid[:], x.rearrange("b (t p) d -> p (b t) d", p=P)).then_inc(loaded, 16)
            sp.wait_ge(loaded, 16)

        @block.vector
        def _(dve):
            nc.vector.memset(g.ident[:], 0.0)
            nc.vector.memset(g.ident_b[:], 0.0)
            nc.vector.memset(g.mask[:], 0.0)
            nc.vector.memset(g.ones[:], 1.0)
            nc.vector.memset(g.eps[:], LN_EPS).then_inc(zeroed, 1)

        @block.gpsimd
        def _(pool):
            pool.wait_ge(zeroed, 1)
            diag = dict(compare_op=ALU.not_equal, fill=1.0, base=0, pattern=[[-1, P]], channel_multiplier=1)
            nc.gpsimd.affine_select(out=g.ident[:], in_=g.ident[:], **diag)
            nc.gpsimd.affine_select(out=g.ident_b[:], in_=g.ident_b[:], **diag)
            nc.gpsimd.affine_select(out=g.mask[:], in_=g.mask[:], compare_op=ALU.is_ge, fill=NEG,
                                    base=0, pattern=[[-1, P]], channel_multiplier=1)
            E = g.rank.shape[1]
            nc.gpsimd.iota(g.rank_i[:], pattern=[[-1, E]], base=E, channel_multiplier=0).then_inc(made, 1)
            pool.wait_ge(made, 1)
            nc.gpsimd.tensor_copy(g.rank[:], g.rank_i[:]).then_inc(made, 1)


class ExpertWeights:

    def __init__(self, c, w1, b1, w2, b2, ws1, bs1, ws2, bs2):
        self.dram = w1, b1, w2, b2, ws1, bs1, ws2, bs2
        self.NE, self.D, self.F = NE, D, F = w1.shape
        self.FB = FB = F // P
        self.N = N = NE + 1
        self.up_hi, self.up_lo = (c.sb(x, [P, N, F], F32R) for x in ("up_hi", "up_lo"))
        self.down_hi, self.down_lo = (c.sb(x, [P, N, FB * D], F32R) for x in ("down_hi", "down_lo"))
        self.b1, self.b2 = c.sb("b1s", [P, N, FB]), c.sb("b2s", [P, N])
        self.loaded = [c.sem(f"w_loaded{s}") for s in range(2)]
        self.bias_loaded, self.hi_ready, self.lo_ready = (c.sem(x) for x in ("bias_l", "w_hi", "w_lo"))

    def load(self, nc, sp, raw):
        w1, b1, w2, b2, ws1, bs1, ws2, bs2 = self.dram
        NE, N, F = self.NE, self.N, self.F
        with nc.allow_non_contiguous_dma(reason="biases, a few KB"):
            sp.dma_start(self.b1[:, 0:NE, :], b1.rearrange("e (f p) -> p e f", p=P)).then_inc(self.bias_loaded, 16)
            sp.dma_start(self.b1[:, NE, :], bs1.rearrange("(f p) -> p f", p=P)).then_inc(self.bias_loaded, 16)
            sp.dma_start(self.b2[:, 0:NE], b2.rearrange("e d -> d e")).then_inc(self.bias_loaded, 16)
            sp.dma_start(self.b2[:, NE:N], bs2.rearrange("(d o) -> d o", o=1)).then_inc(self.bias_loaded, 16)
        for e in range(N):
            if e >= 2:
                sp.wait_ge(self.lo_ready, e - 1)
            s = e % 2
            up, down = (w1[e], w2[e]) if e < NE else (ws1, ws2)
            sp.dma_start(raw[s][:, 0:F], up).then_inc(self.loaded[s], 16)
            sp.dma_start(raw[s][:, F:].rearrange("p (f d) -> p f d", f=self.FB),
                         down.rearrange("(f p) d -> p f d", p=P)).then_inc(self.loaded[s], 16)
        sp.wait_ge(self.bias_loaded, 64)

    def split(self, nc, g, pool, raw):
        F = self.F
        for e in range(self.N):
            s = e % 2
            pool.wait_ge(self.loaded[s], 32 * (e // 2 + 1))
            up, down = raw[s][:, 0:F], raw[s][:, F:]
            pool_copy(nc, g, self.up_hi[:, e], up)
            pool_copy(nc, g, self.down_hi[:, e], down).then_inc(self.hi_ready, 1)
            pool.wait_ge(self.hi_ready, e + 1)
            nc.gpsimd.tensor_tensor(self.up_lo[:, e], up, f32(self.up_hi[:, e]), ALU.subtract)
            nc.gpsimd.tensor_tensor(self.down_lo[:, e], down, f32(self.down_hi[:, e]),
                                    ALU.subtract).then_inc(self.lo_ready, 1)


def layernorm(nc, g, first, wg=None, weights=None):
    with ExitStack() as st:
        c = Ctx(nc, st)
        c.n = g.stage
        T = g.resid.shape[1]
        GT = CH // P
        G = T // GT
        E = g.rank.shape[1]
        moments = c.sb("moments", [P, T, 2])
        std = c.sb("std", [P, T])
        rstd = c.sb("rstd", [P, T])
        U = 4 if G % 4 == 0 else 2
        xn = [c.sb(f"xn{s}", [P, GT, P]) for s in range(U)]
        xT = [c.ps(f"xT{s}", [P, CH]) for s in range(U)]
        stats_done, moments_done, std_done, rstd_done = (c.sem(x) for x in ("stats", "mom", "std", "rstd"))
        xn_ready, xT_ready, hi_ready, lo_ready = (c.sem(x) for x in ("xn_r", "xT_r", "hi_r", "lo_r"))
        if wg is not None:
            raw = [c.sb(f"raw{s}", [P, weights.F + weights.FB * weights.D]) for s in range(2)]
            wg_raw = c.sb("wg_raw", [P, E])
            wgs = c.sb("wgs", [P, 2, E], F32R)
            TH = T // 2
            logits2 = [c.ps(f"logits2{s}", [P, CH // (2 * E), 2, E]) for s in range(2)]
            logits = c.sb("logits", [P, T, E])
            cT = [x[0:E, :] for x in xT]
            work = [c.sb(f"work{s}", [P, T, E]) for s in range(6)]
            col = [c.sb(f"col{s}", [P, T]) for s in range(9)]
            wg_loaded, wg_split = c.sem("wg_l"), c.sem("wg_s")
            lg_ready = c.sem("lg_r")
            chain, z_ready, exp_ready, cw_ready = (c.sem(x) for x in ("chain", "z_r", "exp_r", "cw_r"))
            cwT_ready, cwh_ready, cwl_ready, cw_zeroed, sel_ready = (
                c.sem(x) for x in ("cwT_r", "cwh_r", "cwl_r", "cw_z", "sel_r"))
        block = st.enter_context(nc.Block())

        if wg is not None:
            @block.sync
            def _(sp):
                sp.dma_start(wg_raw[:], wg).then_inc(wg_loaded, 16)
                weights.load(nc, sp, raw)

            @block.gpsimd
            def _(pool):
                nc.gpsimd.memset(f32(g.select[:]), 0.0).then_inc(sel_ready, 1)
                nc.gpsimd.memset(f32(g.cwT[:]), 0.0).then_inc(cw_zeroed, 1)
                pool.wait_ge(sel_ready, 1)
                for k, first in enumerate((0, LO)):
                    nc.gpsimd.affine_select(out=g.select[:], in_=f32(g.select[:]), compare_op=ALU.not_equal,
                                            fill=1.0, base=-first, pattern=[[-1, E], [0, P]],
                                            channel_multiplier=1).then_inc(sel_ready, 1)
                    pool.wait_ge(sel_ready, k + 2)
                weights.split(nc, g, pool, raw)

        @block.vector
        def _(dve):
            give(dve, lo_ready)
            if first:
                with dve.Fori(0, T // 8) as q:
                    row_stats(nc, g, q * 8, 8).then_inc(stats_done, 1)
                dve.wait_ge(stats_done, T // 8)
            for t in range(T):
                last = nc.vector.bn_aggr(moments[:, t, :], g.stats[:, t, :])
            last.then_inc(moments_done, 1)
            dve.wait_ge(std_done, 1)
            nc.vector.reciprocal(rstd[:], std[:]).then_inc(rstd_done, 1)
            dve.wait_ge(rstd_done, 1)
            if wg is not None:
                dve.wait_ge(wg_loaded, 16)
                nc.vector.tensor_copy(wgs[:, 0, :], wg_raw[:]).then_inc(wg_split, 1)
                dve.wait_ge(wg_split, 1)
                nc.vector.tensor_tensor(wgs[:, 1, :], wg_raw[:], f32(wgs[:, 0, :]), ALU.subtract).then_inc(wg_split, 1)
            with dve.Fori(0, G // U) as i:
                dve.wait_ge(xT_ready, i * U + 1)
                for s in range(U + 2):
                    if s < U:
                        for j in range(GT):
                            k = i * (U * GT) + (s * GT + j)
                            last = nc.vector.tensor_scalar(
                                xn[s][:, j, :], g.resid[:, bass.ds(k, 1), :], moments[:, bass.ds(k, 1), 0:1],
                                rstd[:, bass.ds(k, 1)], ALU.subtract, ALU.mult)
                        last.then_inc(xn_ready, 1)
                    if s >= 2:
                        dve.wait_ge(hi_ready, i * U + (s - 1))
                        at = bass.ds(i * (U * CH) + (s - 2) * CH, CH)
                        nc.vector.tensor_tensor(g.xl[:, at], xT[s - 2][:], f32(g.xh[:, at]),
                                                ALU.subtract).then_inc(lo_ready, 1)
            if wg is None:
                return

            n = [0]

            def link(ins):
                n[0] += 1
                ins.then_inc(chain, 1)
                dve.wait_ge(chain, n[0])

            def over(a):
                return a.unsqueeze(2).to_broadcast([P, TH, E])

            tt, red = nc.vector.tensor_tensor, nc.vector.tensor_reduce
            rank = g.rank[:].unsqueeze(1).to_broadcast([P, TH, E])

            def route(half):
                at = slice(half * TH, (half + 1) * TH)
                lg, z, e, w2, eq, s1, s2 = (x[:, at, :] for x in [logits] + work)
                mx, se, rs, v1, k1, v2, k2, den, rden = (x[:, at] for x in col)
                dve.wait_ge(lg_ready, half + 1)
                link(nc.vector.tensor_copy(lg, logits2[half][:, 0:TH, 0, :]))
                link(tt(lg, lg, logits2[half][:, 0:TH, 1, :], ALU.add))
                link(red(mx, lg, AX_X, ALU.max))
                tt(z, lg, over(mx), ALU.subtract).then_inc(z_ready, 1)
                dve.wait_ge(exp_ready, half + 1)
                link(red(se, e, AX_X, ALU.add))
                link(nc.vector.reciprocal(rs, se))
                link(tt(z, e, over(rs), ALU.mult))
                link(red(v1, z, AX_X, ALU.max))
                link(tt(eq, z, over(v1), ALU.is_equal))
                link(tt(w2, eq, rank, ALU.mult))
                link(red(k1, w2, AX_X, ALU.max))
                link(tt(s1, w2, over(k1), ALU.is_equal))
                link(nc.vector.scalar_tensor_tensor(eq, s1, -2.0, z, ALU.mult, ALU.add))
                link(red(v2, eq, AX_X, ALU.max))
                link(tt(w2, eq, over(v2), ALU.is_equal))
                link(tt(eq, w2, rank, ALU.mult))
                link(red(k2, eq, AX_X, ALU.max))
                link(tt(s2, eq, over(k2), ALU.is_equal))
                link(tt(den, v1, v2, ALU.add))
                link(nc.vector.tensor_scalar(se, den, TOPK_EPS, None, ALU.add))
                link(nc.vector.reciprocal(rden, se))
                link(nc.vector.tensor_scalar(den, rden, HALF, None, ALU.mult))
                link(tt(w2, s1, s2, ALU.add))
                link(tt(eq, w2, z, ALU.mult))
                tt(w2, eq, over(den), ALU.mult).then_inc(cw_ready, 1)

            route(0)
            route(1)
            for q in range(G):
                dve.wait_ge(cwh_ready, q + 1)
                at = slice(q * CH, (q + 1) * CH)
                nc.vector.tensor_tensor(g.cwT[LO:LO + E, at], cT[q % U], f32(g.cwT[0:E, at]), ALU.subtract).then_inc(cwl_ready, 1)

        @block.scalar
        def _(act):
            act.wait_ge(moments_done, 1)
            nc.scalar.activation(std[:], moments[:, :, 1], ACT.Sqrt, bias=g.eps[:]).then_inc(std_done, 1)
            with act.Fori(0, G // U) as i:
                for s in range(U):
                    act.wait_ge(xT_ready, i * U + (s + 1) + 1)
                    nc.scalar.activation(g.xh[:, bass.ds(i * (U * CH) + s * CH, CH)], xT[s][:], ACT.Copy).then_inc(hi_ready, 1)
            if wg is None:
                return
            act.wait_ge(cw_zeroed, 1)
            for half in range(2):
                act.wait_ge(z_ready, half + 1)
                at = slice(half * TH, (half + 1) * TH)
                nc.scalar.activation(work[1][:, at, :], work[0][:, at, :], ACT.Exp).then_inc(exp_ready, 1)
            for q in range(G):
                act.wait_ge(cwT_ready, q + 1)
                nc.scalar.activation(g.cwT[0:E, q * CH:(q + 1) * CH], cT[q % U], ACT.Copy).then_inc(cwh_ready, 1)

        @block.tensor
        def _(pe):
            give(pe, xT_ready)
            if wg is not None:
                pe.wait_ge(wg_split, 2)
            with pe.Fori(0, G // U) as i:
                pe.wait_ge(lo_ready, i * U + 1)
                for s in range(U):
                    pe.wait_ge(xn_ready, i * U + (s + 1))
                    for j in range(GT):
                        last = nc.tensor.transpose(xT[s][:, j * P:(j + 1) * P], xn[s][:, j, :], g.ident[:])
                    last.then_inc(xT_ready, 1)
            if wg is None:
                return
            pe.wait_ge(lo_ready, G + 1)
            for t in range(T):
                at = slice(t * P, (t + 1) * P)
                out = logits2[t // TH][:, t % TH]
                nc.tensor.matmul(out, g.xh[:, at], wgs[:], start=True, stop=False)
                last = nc.tensor.matmul(out[:, 0, :], g.xl[:, at], wgs[:, 0, :], start=False, stop=True)
                if (t + 1) % TH == 0:
                    last.then_inc(lg_ready, 1)
            for q in range(G):
                if q % (G // 2) == 0:
                    pe.wait_ge(cw_ready, q // (G // 2) + 1)
                if q >= U:
                    pe.wait_ge(cwl_ready, q - U + 1)
                for j in range(GT):
                    last = nc.tensor.transpose(cT[q % U][:, j * P:(j + 1) * P], work[2][:, q * GT + j, :], g.ident[:])
                last.then_inc(cwT_ready, 1)


def moe(nc, g, weights, stats_too):
    with ExitStack() as st:
        c = Ctx(nc, st)
        c.n = g.stage
        NE, N, FB = weights.NE, weights.N, weights.FB
        T = g.resid.shape[1]
        GT = CH // P
        G = T // GT
        w1h, w1l, w2h, w2l = weights.up_hi, weights.up_lo, weights.down_hi, weights.down_lo
        b1s, b2s = weights.b1, weights.b2
        act_f = [c.sb(f"act_f{f}", [P, CH]) for f in range(FB)]
        act_h = [[c.sb(f"act_h{s}{f}", [P, CH], F32R) for f in range(FB)] for s in range(2)]
        act_l = [[c.sb(f"act_l{s}{f}", [P, CH], F32R) for f in range(FB)] for s in range(2)]
        cwb = c.sb("cwb", [P, CH])
        yw = [c.sb(f"yw{s}", [P, CH]) for s in range(2)]
        acc = c.sb("acc", [P, CH])
        hp = [c.ps(f"hp{f}", [P, CH]) for f in range(FB)]
        yp = [c.ps(f"yp{s}", [P, CH]) for s in range(2)]
        cp = c.ps("cp", [P, CH])
        tp = c.ps("tp", [P, GT, P])
        names = ("h_r", "silu_r", "lo_r", "y_r", "cp_r", "cwb_r", "yw_r",
                 "acc_r", "tp_r", "res_r")
        (h_ready, silu_ready, lo_ready, y_ready, cp_ready, cwb_ready,
         yw_ready, acc_ready, tp_ready, resid_ready) = (c.sem(x) for x in names)
        block = st.enter_context(nc.Block())

        def after(eng, sem, count):
            if not isinstance(count, int) or count > 0:
                eng.wait_ge(sem, count)

        def tiles(eng, tile):
            tile(0, 0, False)
            if G > 2:
                with eng.Fori(0, (G - 2) // 2) as i:
                    tile(i * 2 + 1, 1, False)
                    tile(i * 2 + 2, 0, False)
            tile(G - 1, 1, True)

        assert N % 2 == 1 and G % 2 == 0

        @block.gpsimd
        def _(pool):
            def tile(t, par, last):
                for e in range(N):
                    n, s = t * N + e, (par + e) % 2
                    pool.wait_ge(yw_ready, n + 1)
                    if e == 0:
                        after(pool, tp_ready, t)
                        pool_copy(nc, g, acc[:], yw[s][:]).then_inc(acc_ready, 1)
                    else:
                        pool.wait_ge(acc_ready, n)
                        nc.gpsimd.tensor_tensor(acc[:], acc[:], yw[s][:], ALU.add).then_inc(acc_ready, 1)

            tiles(pool, tile)

        @block.vector
        def _(dve):
            def low_halves(n, s):
                for f in range(FB):
                    dve.wait_ge(silu_ready, n * FB + (f + 1))
                    nc.vector.tensor_tensor(act_l[s][f][:], act_f[f][:], f32(act_h[s][f][:]),
                                            ALU.subtract).then_inc(lo_ready, 1)

            def combine_weights(n, m):
                dve.wait_ge(cp_ready, m + 1)
                after(dve, yw_ready, n)
                nc.vector.tensor_copy(cwb[:], cp[:]).then_inc(cwb_ready, 1)

            def residual(t):
                dve.wait_ge(tp_ready, t + 1)
                at = bass.ds(t * GT, GT)
                nc.vector.tensor_tensor(g.resid[:, at, :], tp[:], g.resid[:, at, :], ALU.add).then_inc(resid_ready, 1)
                if stats_too:
                    dve.wait_ge(resid_ready, t + 1)
                    row_stats(nc, g, t * GT, GT)

            def tile(t, par, last):
                for e in range(N):
                    n, m, s = t * N + e, t * NE + e, (par + e) % 2
                    if e < N - 1 or not last:
                        low_halves(n + 1, 1 - s)
                    if e == 0 and not (isinstance(t, int) and t == 0):
                        residual(t - 1)
                    dve.wait_ge(y_ready, n + 1)
                    after(dve, acc_ready, n - 1)
                    if e < NE:
                        dve.wait_ge(cwb_ready, m + 1)
                        nc.vector.scalar_tensor_tensor(yw[s][:], yp[s][:], b2s[:, e:e + 1], cwb[:], ALU.add,
                                                       ALU.mult).then_inc(yw_ready, 1)
                    else:
                        nc.vector.tensor_scalar(yw[s][:], yp[s][:], b2s[:, e:e + 1], HALF * SHARED_SCALE, ALU.add,
                                                ALU.mult).then_inc(yw_ready, 1)
                    if e < NE - 1:
                        combine_weights(n + 1, m + 1)
                    elif e == N - 1 and not last:
                        combine_weights(n + 1, m)

            low_halves(0, 0)
            combine_weights(0, 0)
            tiles(dve, tile)
            residual(G - 1)

        @block.scalar
        def _(act):
            def tile(t, par, last):
                for e in range(N):
                    n, s = t * N + e, (par + e) % 2
                    for f in range(FB):
                        act.wait_ge(h_ready, n * FB + (f + 1))
                        after(act, y_ready, n - 1)
                        after(act, lo_ready, (n - 1) * FB + (f + 1))
                        bias = b1s[:, e, f:f + 1]
                        nc.scalar.activation(act_h[s][f][:], hp[f][:], ACT.Silu, bias=bias)
                        nc.scalar.activation(act_f[f][:], hp[f][:], ACT.Silu, bias=bias).then_inc(silu_ready, 1)

            tiles(act, tile)

        @block.tensor
        def _(pe):
            def up(t, e):
                n, m, at = t * N + e, t * NE + e, bass.ds(t * CH, CH)
                for f in range(FB):
                    after(pe, silu_ready, (n - 1) * FB + (f + 1))
                    cols = slice(f * P, (f + 1) * P)
                    nc.tensor.matmul(hp[f][:], w1h[:, e, cols], g.xh[:, at], start=True, stop=False)
                    nc.tensor.matmul(hp[f][:], w1h[:, e, cols], g.xl[:, at], start=False, stop=False)
                    nc.tensor.matmul(hp[f][:], w1l[:, e, cols], g.xh[:, at], start=False, stop=True).then_inc(h_ready, 1)
                if e < NE:
                    after(pe, cwb_ready, m)
                    nc.tensor.matmul(cp[:], g.select[:, e, :], g.cwT[:, at], start=True, stop=True).then_inc(cp_ready, 1)

            def down(t, e, s):
                n = t * N + e
                after(pe, yw_ready, n - 1)
                for f in range(FB):
                    rows = slice(f * P, (f + 1) * P)
                    pe.wait_ge(lo_ready, n * FB + (f + 1))
                    nc.tensor.matmul(yp[s][:], w2h[:, e, rows], act_h[s][f][:], start=f == 0, stop=False)
                    nc.tensor.matmul(yp[s][:], w2l[:, e, rows], act_h[s][f][:], start=False, stop=False)
                    last = nc.tensor.matmul(yp[s][:], w2h[:, e, rows], act_l[s][f][:], start=False, stop=f == FB - 1)
                last.then_inc(y_ready, 1)

            def back(t):
                pe.wait_ge(acc_ready, t * N + N)
                after(pe, resid_ready, t)
                for j in range(GT):
                    last = nc.tensor.transpose(tp[:, j, :], acc[:, j * P:(j + 1) * P], g.ident[:])
                last.then_inc(tp_ready, 1)

            def tile(t, par, last):
                for e in range(N):
                    if e < N - 1:
                        up(t, e + 1)
                    elif not last:
                        up(t + 1, 0)
                    if e == 0 and not (isinstance(t, int) and t == 0):
                        back(t - 1)
                    down(t, e, (par + e) % 2)

            up(0, 0)
            tiles(pe, tile)
            back(G - 1)


def attention(nc, g, wq, wk, wv, wo, bo, S, stats_too):
    with ExitStack() as st:
        c = Ctx(nc, st)
        c.n = g.stage
        D, H, C = wq.shape
        T = g.resid.shape[1]
        B = T * P // S
        NP = H // 2
        ST = S // P
        NC = S // CH
        QT = CH // P
        NPR = 4
        NRING = 3
        SCALE = float(C) ** -0.5
        WC = NP * P // CH

        wvh, wvl = (c.sb(x, [P, NP * P], F32R) for x in ("wvh", "wvl"))
        wo_sb = c.sb("wo_sb", [P, NP, D])
        bo_sb = c.sb("bo_sb", [P, 1])
        wraw = c.sb("wraw", [P, 2, P])
        wh, wl = ([c.sb(f"{x}{s}", [P, 2, 2, 2, C], F32R) for s in range(2)] for x in ("wh", "wl"))
        K1, K2, Q1, Q2 = ([[c.sb(f"{x}{s}{a}", [P, S], F32R) for a in range(2)] for s in range(2)]
                          for x in ("K1", "K2", "Q1", "Q2"))
        xbh, xbl = (Q1[1][a][:] for a in range(2))
        VZ = c.sb("VZ", [P, NP, S])
        Vs = [c.sb(f"Vs{s}", [P, ST, P]) for s in range(2)]
        Pr = [c.sb(f"Pr{s}", [P, 2, CH]) for s in range(NPR)]
        pacc = [c.sb(f"pacc{k}", [P, 2, CH]) for k in range(NC)]
        nmax2 = [c.sb(f"nmax2{a}", [P, 2, ST]) for a in range(2)]
        nmax = [c.sb(f"nmax{a}", [P, ST]) for a in range(2)]
        diag = [c.sb(f"diag{k}", [P, QT, P], F32R) for k in range(NC)]
        row64 = c.sb("row64", [P, P], F32R)
        ssum = [pacc[0][:, 0, :], c.sb("ssum1", [P, CH])[:]]
        zinv = [pacc[0][:, 1, :], c.sb("zinv1", [P, CH])[:]]
        oT = [Pr[NPR - NC + k][:, 0, :] for k in range(NC)]

        sc = [c.ps(f"sc{s}", [P, 2, CH]) for s in range(2)]
        ring = [c.ps(f"ring{s}", [P, CH]) for s in range(NRING)]
        zp = c.ps("zp", [P, CH])
        outT = zp, ring[0]

        (wv_loaded, w_loaded, w_split, wv_split, w_free, ring_ready, ring_free, hi_ready, k2_ready, nm_ready,
         diag_ready, sc_ready, p_ready, pv_ready, zinv_ready, z_ready, z_taken, xb_ready, v_ready, v_copied,
         vs_ready, padd1_ready, padd0_ready, ln_ready, newton, o_ready, ob_ready, ot_ready, resid_ready, set_ready) = (
            c.sem(x) for x in (
                "wv_l", "w_l", "w_s", "wv_s", "w_f", "ring_r", "ring_f", "hi_r", "k2_r", "nm_r",
                "diag_r", "sc_r", "p_r", "pv_r", "zi_r", "z_r", "z_t", "xb_r", "v_r", "v_c",
                "vs_r", "padd1_r", "padd0_r", "ln_r", "newton", "o_r", "ob_r", "ot_r", "res_r", "set_r"))

        ORDER = list(range(NC))[::-1]
        proj = [("proj", a, m, k) for a in range(2) for m in range(2) for k in range(NC)]
        spans = []
        for t in range(ST):
            for half in range(-(-P * (t + 1) // CH)):
                spans.append((t, half, min(CH, P * (t + 1) - CH * half)))
        maxes = [[("max", a, *x) for x in spans] for a in range(2)]
        rows = [[("row", a, k) for k in ORDER] for a in range(2)]
        jobs = proj[:2 * NC]
        for i, x in enumerate(proj[2 * NC:]):
            jobs += [x] + maxes[0][2 * i:2 * i + 2]
        jobs += maxes[0][4 * NC:] + maxes[1][:4] + rows[0] + maxes[1][4:] + rows[1]
        NJ = len(jobs)

        def begins(k, kt):
            q0 = max(CH * k, P * kt)
            return q0, CH * (k + 1) - q0

        steps = [(k, kt) for k in ORDER for kt in range(QT * (k + 1))]
        NS = len(steps)
        N1 = QT * NC
        N0 = NS - N1
        assert NS % 2 == 0 and NS % NPR == 0 and NC == 2 and N0 == NPR
        NEXTS = NJ - NC
        load = [0 if i == 0 else 2 * begins(*steps[i])[1] + 4 * begins(*steps[i - 1])[1] for i in range(NS)]
        per = [min(NEXTS, NEXTS * sum(load[:i]) // sum(load[:NS - 2])) for i in range(NS + 1)]
        slots = [[jobs[n] for n in range(per[i], per[i + 1])] for i in range(NS)]
        SUM0, SUM1 = (("sum", 0, k) for k in range(NC))
        slots[N1 + 1].append(SUM1)
        slots.append(jobs[NEXTS:] + [SUM0])
        flat = [x for slot in slots for x in slot]
        begin = [sum(len(x) for x in slots[:i]) for i in range(NS + 2)]
        before = [len(x) // 2 if i else 0 for i, x in enumerate(slots)]
        NL = len(flat)

        def ring_count(u, n):
            return u * NL + (NJ + n)

        def since(n, looped):
            if n >= NRING:
                return NRING
            if not looped:
                return None
            return next(n + NL - i for i in range(NL)[::-1] if i % NRING == n)

        def first_count(x):
            return jobs.index(x) + 1

        def loop_count(u):
            return lambda x: ring_count(u, flat.index(x) + 1)

        NPROJ, NROW = len(proj), len(rows) * NC

        block = st.enter_context(nc.Block())

        @block.sync
        def _(sp):
            wkq = [w.rearrange("d (p h) c -> d p (h c)", h=2) for w in (wk, wq)]
            for m in range(2):
                sp.dma_start(wraw[:, m, :], wkq[m][:, 0, :]).then_inc(w_loaded, 16)
            sp.dma_start(VZ[:, 0:NP * P // S, :].rearrange("p a b -> p (a b)"),
                         wv.rearrange("d h c -> d (h c)")).then_inc(wv_loaded, 16)
            for a in range(2):
                sp.dma_start(wo_sb[a * C:(a + 1) * C, :, :],
                             wo.rearrange("c (p two) d -> two c p d", two=2)[a]).then_inc(wv_loaded, 16)
            with nc.allow_non_contiguous_dma(reason="a bias, 512 bytes"):
                sp.dma_start(bo_sb[:], bo.rearrange("(d o) -> d o", o=1)).then_inc(wv_loaded, 16)
            with sp.Fori(0, B * NP + 1) as u:
                sp.wait_ge(w_free, u + 1)
                n = (u + 1) % NP
                for m in range(2):
                    sp.dma_start(wraw[:, m, :], wkq[m][:, bass.ds(n, 1), :]).then_inc(w_loaded, 16)
            sp.wait_ge(w_loaded, 32 * (B * NP + 2))

        @block.gpsimd
        def _(pool):
            give(pool, vs_ready)
            def split(n, s):
                pool.wait_ge(w_loaded, n * 32 + 32)
                for a in range(2):
                    for m in range(2):
                        src = wraw[:, m, a * C:(a + 1) * C].unsqueeze(1).to_broadcast([P, 2, C])
                        pool_copy(nc, g, wh[s][:, a, m], src).then_inc(w_split, 1)
                pool.wait_ge(w_split, n * 4 + 4)
                for a in range(2):
                    for m in range(2):
                        src = wraw[:, m, a * C:(a + 1) * C].unsqueeze(1).to_broadcast([P, 2, C])
                        last = nc.gpsimd.tensor_tensor(wl[s][:, a, m], src, f32(wh[s][:, a, m]), ALU.subtract)
                        if (a, m) == (1, 1):
                            last.then_inc(w_free, 1)

            def keys(u1, s, a):
                for k in range(NC):
                    pool.wait_ge(hi_ready, u1 * NPROJ + (a * 2 * NC + k + 1))
                    at = slice(k * CH, (k + 1) * CH)
                    pool_copy(nc, g, K2[s][a][0:C, at], f32(K1[s][a][0:C, at])).then_inc(k2_ready, 1)

            split(0, 0)
            split(1, 1)
            pool.wait_ge(w_free, 2)
            keys(0, 0, 0)
            keys(0, 0, 1)
            with pool.Fori(0, B) as b:
                pool.wait_ge(v_copied, b * (ST * WC) + ST * WC)
                pool.wait_ge(k2_ready, b * (NP * 2 * NC) + 2 * NC)
                pool_copy(nc, g, Vs[0][:].rearrange("p t c -> p (t c)"), VZ[:, 0, :]).then_inc(vs_ready, 1)
                with pool.Fori(0, NP // 2) as ppq:
                    pp = ppq * 2
                    for j in range(2):
                        u = b * NP + pp + j
                        for s, (k, kt) in enumerate(steps):
                            if s < N1:
                                q0, w = begins(k, kt)
                                pool.wait_ge(p_ready, u * NS + (s + 3))
                                new, old = Pr[s % NPR][:, :, 0:w], pacc[k][:, :, CH - w:CH]
                                if kt == 0:
                                    pool.wait_ge(ring_ready, ring_count(u, flat.index(("sum", 0, k)) + 1 - NL))
                                    pool_copy(nc, g, old, new).then_inc(padd1_ready, 1)
                                else:
                                    pool.wait_ge(padd1_ready, u * N1 + s)
                                    nc.gpsimd.tensor_tensor(old, old, new, ALU.add).then_inc(padd1_ready, 1)
                            if s in (3, 5):
                                pool.wait_ge(padd1_ready, u * N1 + (s + 1))
                                keys(u + 1, 1 - j, (s - 3) // 2)
                                pool.wait_ge(k2_ready, u * (2 * NC) + (2 * NC + (s - 1) // 2 * NC))
                            if s == 1:
                                pool.wait_ge(pv_ready, u * NS + NPR)
                                if j == 0:
                                    nxt = pp + 1
                                else:
                                    nxt = (pp + 2) % NP
                                    pool.wait_ge(z_ready, u * NC + 2)
                                pool_copy(nc, g, Vs[1 - j][:].rearrange("p t c -> p (t c)"),
                                          VZ[:, bass.ds(nxt, 1), :].rearrange("p a c -> p (a c)")).then_inc(vs_ready, 1)
                                split(u + 2, j)

        def vs_count(b, pair):
            return b * (NP + 1) + pair + 1

        @block.vector
        def _(dve):
            give(dve, z_ready, z_ready, resid_ready, *[padd0_ready] * NPR)
            nc.vector.memset(f32(row64[:]), 0.0).then_inc(set_ready, 1)
            dve.wait_ge(set_ready, 1)
            nc.vector.memset(f32(row64[:, C:C + 1]), 1.0)
            for s in range(2):
                for a in range(2):
                    nc.vector.memset(f32(K2[s][a][C:P, :]), 1.0)
            nc.vector.memset(nmax2[0][:], 3e38)
            nc.vector.memset(nmax2[1][:], 3e38).then_inc(set_ready, 1)
            dve.wait_ge(wv_loaded, 64)
            raw_v = VZ[:, 0:NP * P // S, :].rearrange("p a b -> p (a b)")
            nc.vector.tensor_copy(wvh[:], raw_v).then_inc(wv_split, 1)
            dve.wait_ge(wv_split, 1)
            nc.vector.tensor_tensor(wvl[:], raw_v, f32(wvh[:]), ALU.subtract).then_inc(wv_split, 1)
            dve.wait_ge(set_ready, 2)

            def job(u1, s, x, count_of):
                what, a = x[:2]
                count = count_of(x)
                dve.wait_ge(ring_ready, count)
                if what == "proj":
                    m, k = x[2:]
                    at = slice(k * CH, (k + 1) * CH)
                    dve.wait_ge(hi_ready, u1 * NPROJ + (proj.index(x) + 1))
                    if m == 0:
                        nc.vector.tensor_tensor(K1[s][a][C:P, at], bank[C:P, :], f32(K1[s][a][C:P, at]),
                                                ALU.subtract).then_inc(ring_free, 1)
                    else:
                        nc.vector.tensor_tensor(Q2[s][a][0:C, at], bank[0:C, :], f32(Q1[s][a][0:C, at]),
                                                ALU.subtract).then_inc(ring_free, 1)
                elif what == "sum":
                    nc.vector.tensor_copy(ssum[x[2]], bank[:]).then_inc(ring_free, 1)
                elif what == "max":
                    t, half, w = x[2:]
                    nc.vector.tensor_reduce(nmax2[a][:, half, t:t + 1], bank[:, 0:w], AX_X, ALU.max,
                                            negate=True).then_inc(ring_free, 1)
                    if (t, half) == spans[-1][:2]:
                        dve.wait_ge(ring_free, count)
                        nc.vector.tensor_tensor(nmax[a][:], nmax2[a][:, 0, :], nmax2[a][:, 1, :], ALU.min).then_inc(nm_ready, 1)
                        dve.wait_ge(nm_ready, u1 * 2 + (a + 1))
                        for k in ORDER:
                            nc.vector.tensor_tensor(
                                diag[k][:], g.ident[:].unsqueeze(1).to_broadcast([P, QT, P]),
                                nmax[a][:, k * QT:(k + 1) * QT].unsqueeze(2).to_broadcast([P, QT, P]),
                                ALU.mult).then_inc(diag_ready, 1)
                else:
                    k = x[2]
                    nc.vector.tensor_copy(Q2[s][a][C:P, k * CH:(k + 1) * CH], bank[C:P, :]).then_inc(ring_free, 1)

            for n in range(NJ):
                bank = ring[n % NRING]
                job(0, 0, jobs[n], first_count)
            def batch_x(b):
                nc.vector.tensor_copy(xbh, f32(g.xh[:, bass.ds(b * S, S)]))
                nc.vector.tensor_copy(xbl, f32(g.xl[:, bass.ds(b * S, S)])).then_inc(xb_ready, 1)

            batch_x(0)
            with dve.Fori(0, B) as b:
                with dve.Fori(0, NP // 2) as ppq:
                    pp = ppq * 2
                    for j in range(2):
                        u = b * NP + pp + j

                        def over_sums(k):
                            i = ORDER.index(k)
                            dve.wait_ge(z_taken, u * NC + (i + 2))
                            dve.wait_ge(zinv_ready, u * NC + (i + 1))
                            z = VZ[:, bass.ds(pp + j, 1), k * CH:(k + 1) * CH]
                            nc.vector.tensor_tensor(z, z, zinv[k], ALU.mult)
                            nc.vector.scalar_tensor_tensor(ssum[k], ssum[k], -1.0, zinv[k], ALU.mult,
                                                           ALU.mult).then_inc(newton, 1)

                        def corrected(k):
                            z = VZ[:, bass.ds(pp + j, 1), k * CH:(k + 1) * CH]
                            dve.wait_ge(newton, u * NC + (ORDER.index(k) + 1))
                            nc.vector.scalar_tensor_tensor(z, ssum[k], 2.0, z, ALU.add, ALU.mult).then_inc(z_ready, 1)

                        def add(i):
                            w = begins(*steps[i])[1]
                            new, old = Pr[i % NPR][:, :, 0:w], pacc[0][:, :, CH - w:CH]
                            dve.wait_ge(p_ready, u * NS + (i + 3))
                            if i == N1:
                                nc.vector.tensor_copy(old, new).then_inc(padd0_ready, 1)
                            else:
                                dve.wait_ge(padd0_ready, u * N0 + (i - N1 + NPR))
                                nc.vector.tensor_tensor(old, old, new, ALU.add).then_inc(padd0_ready, 1)

                        for i, slot in enumerate(slots):
                            for n, x in enumerate(slot, begin[i]):
                                if i == NS and x == SUM0:
                                    add(NS - 1)
                                    over_sums(1)
                                bank = ring[n % NRING]
                                job(u + 1, 1 - j, x, loop_count(u))
                            if N1 <= i < NS - 1:
                                add(i)
                        corrected(1)
                        over_sums(0)
                        corrected(0)
                batch_x((b + 1) % B)
                for k in range(NC):
                    dve.wait_ge(o_ready, b * NC + (k + 1) + 1)
                    nc.vector.tensor_scalar(oT[k], sc[1][:, k, :], bo_sb[:], None, ALU.add).then_inc(ob_ready, 1)
                for k in range(NC):
                    dve.wait_ge(ot_ready, b * NC + (k + 1) + 1)
                    at = bass.ds(b * ST + k * QT, QT)
                    nc.vector.tensor_tensor(g.resid[:, at, :], outT[k][:].rearrange("p (t d) -> p t d", d=P),
                                            g.resid[:, at, :], ALU.add).then_inc(resid_ready, 1)
                if stats_too:
                    dve.wait_ge(resid_ready, b * NC + (NC + 1))
                    row_stats(nc, g, b * ST, ST)

        @block.scalar
        def _(act):
            give(act, p_ready, p_ready, z_taken)
            nc.scalar.preload_act_table_set("natural_log_exp_and_others")

            def job(s, n, x, count):
                _, a, m, k = x
                act.wait_ge(ring_ready, count)
                dst = (K1 if m == 0 else Q1)[s][a]
                nc.scalar.activation(dst[:, k * CH:(k + 1) * CH], ring[n % NRING][:], ACT.Copy).then_inc(hi_ready, 1)

            def exponential(u, s):
                act.wait_ge(sc_ready, u * NS + (s + 1))
                act.wait_ge(pv_ready, u * NS + (s + 1))
                if s < NPR:
                    act.wait_ge(padd0_ready, u * N0 + (s + 1))
                else:
                    act.wait_ge(padd1_ready, u * N1 + (s - NPR + 1))
                w = begins(*steps[s])[1]
                nc.scalar.activation(Pr[s % NPR][:, :, 0:w], sc[s % 2][:, :, 0:w], ACT.Exp,
                                     scale=SCALE).then_inc(p_ready, 1)

            for n, x in enumerate(jobs):
                if x[0] == "proj":
                    job(0, n, x, n + 1)
            exponential(0, 0)
            with act.Fori(0, B) as b:
                act.wait_ge(o_ready, b * NC + 1)
                act.wait_ge(vs_ready, b * (NP + 1) + 1)
                act.wait_ge(wv_split, 2)
                for t in range(ST):
                    for w in range(WC):
                        act.wait_ge(v_ready, b * (ST * WC) + (t * WC + w + 1) + 1)
                        n = CH // P
                        nc.scalar.activation(VZ[:, w * n:(w + 1) * n, t * P:(t + 1) * P],
                                             sc[1][:, w % 2, :].rearrange("p (a c) -> p a c", c=P),
                                             ACT.Copy).then_inc(v_copied, 1)
                with act.Fori(0, NP // 2) as ppq:
                    pp = ppq * 2
                    for j in range(2):
                        u = b * NP + pp + j

                        def take(k):
                            done = sum(1 for x in steps if x[0] >= k)
                            act.wait_ge(pv_ready, u * NS + (done + NPR))
                            nc.scalar.activation(VZ[:, bass.ds(pp + j, 1), k * CH:(k + 1) * CH], zp[:],
                                                 ACT.Copy).then_inc(z_taken, 1)

                        def inverse(k):
                            n = flat.index(("sum", 0, k))
                            act.wait_ge(ring_free, ring_count(u, n + 1))
                            nc.scalar.activation(zinv[k], ssum[k], ACT.Ln).then_inc(ln_ready, 1)
                            act.wait_ge(ln_ready, u * NC + (NC - k))
                            nc.scalar.activation(zinv[k], zinv[k], ACT.Exp, scale=-1.0).then_inc(zinv_ready, 1)

                        def projections(first, end):
                            for i in range(first, end):
                                if slots[s][i][0] == "proj":
                                    job(1 - j, begin[s] + i, slots[s][i], ring_count(u, begin[s] + i + 1))

                        for s in range(NS):
                            projections(0, before[s])
                            if s == NPR - NC:
                                act.wait_ge(ot_ready, b * NC + 1)
                            if s:
                                exponential(u, s)
                            if s == N1:
                                take(1)
                            projections(before[s], len(slots[s]))
                        inverse(1)
                        take(0)
                        exponential(u + 1, 0)
                        inverse(0)

        @block.tensor
        def _(pe):
            mm = nc.tensor.matmul
            give(pe, *[pv_ready] * NPR, v_ready, o_ready, ot_ready)
            pe.wait_ge(set_ready, 2)

            def job(u1, s, n, x, count_of):
                what, a = x[:2]
                count, bank = count_of(x), ring[n % NRING]
                back = since(n, not isinstance(count, int))
                if back:
                    pe.wait_ge(ring_free, count - back)
                if what == "sum":
                    k = x[2]
                    if k == 1:
                        pe.wait_ge(padd1_ready, (u1 - 1) * N1 + N1)
                    else:
                        pe.wait_ge(padd0_ready, (u1 - 1) * N0 + (N0 + NPR))
                    for a in range(2):
                        last = mm(bank[a * C:(a + 1) * C, :], g.ones[:], pacc[k][:, a, :], start=True, stop=True)
                    last.then_inc(ring_ready, 1)
                elif what == "proj":
                    m, k = x[2:]
                    if (a, m, k) == (0, 0, 0):
                        pe.wait_ge(w_free, u1 + 1)
                    h, l = (w[s][:, a, m].rearrange("p r c -> p (r c)") for w in (wh, wl))
                    at = bass.ds(((u1 // NP) % B) * S + k * CH, CH)
                    mm(bank[:], h, g.xh[:, at], start=True, stop=False)
                    mm(bank[:], h, g.xl[:, at], start=False, stop=False)
                    mm(bank[:], l, g.xh[:, at], start=False, stop=True).then_inc(ring_ready, 1)
                elif what == "max":
                    t, half, w = x[2:]
                    if t == 0:
                        pe.wait_ge(ring_free, count_of(("proj", a, 1, NC - 1)))
                    diagonal = CH * half + w == P * (t + 1)
                    last = mm(bank[:, 0:w], Q1[s][a][:, t * P:(t + 1) * P], K1[s][a][:, half * CH:half * CH + w],
                              start=True, stop=not diagonal)
                    if diagonal:
                        last = mm(bank[:, w - P:w], g.ident_b[:], g.mask[:], start=False, stop=True)
                    last.then_inc(ring_ready, 1)
                else:
                    k = x[2]
                    pe.wait_ge(diag_ready, u1 * NROW + (a * NC + ORDER.index(k) + 1))
                    mm(bank[:], row64[:], diag[k][:].rearrange("p t q -> p (t q)"), start=True,
                       stop=True).then_inc(ring_ready, 1)

            def scores(u, s_, slot):
                k, kt = steps[s_]
                q0, w = begins(k, kt)
                pe.wait_ge(p_ready, u * NS + s_ + 1)
                if s_ == 0:
                    pe.wait_ge(ring_free, ring_count(u, 0) - (0 if isinstance(u, int) else 2))
                    pe.wait_ge(k2_ready, u * (2 * NC) + 2 * NC)
                for a in range(2):
                    out = sc[s_ % 2][:, a, 0:w]
                    kk = slice(kt * P, (kt + 1) * P)
                    qq = slice(q0, q0 + w)
                    mm(out, K1[slot][a][:, kk], Q1[slot][a][:, qq], start=True, stop=False)
                    if kt >= QT * k:
                        mm(sc[s_ % 2][:, a, 0:P], g.mask[:], g.ident_b[:], start=False, stop=False)
                    last = mm(out, K2[slot][a][:, kk], Q2[slot][a][:, qq], start=False, stop=True)
                    if a == 1:
                        last.then_inc(sc_ready, 1)
                    yield

            def values(u, s_, slot, b, pair):
                k, kt = steps[s_]
                q0, w = begins(k, kt)
                pe.wait_ge(p_ready, u * NS + (s_ + 3))
                if s_ == 0:
                    pe.wait_ge(vs_ready, vs_count(b, pair) + 1)
                if kt == 0:
                    pe.wait_ge(z_taken, u * NC + (NC - k))
                first, end = kt == 0, kt == QT * (k + 1) - 1
                for a in range(2):
                    last = mm(zp[a * C:(a + 1) * C, q0 - CH * k:CH], Vs[slot][:, kt, a * C:(a + 1) * C],
                              Pr[s_ % NPR][:, a, 0:w], start=first, stop=end)
                    if a == 1:
                        last.then_inc(pv_ready, 1)
                    yield

            for n in range(NJ):
                job(0, 0, n, jobs[n], first_count)
            for _ in scores(0, 0, 0):
                pass
            with pe.Fori(0, B) as b:
                pe.wait_ge(xb_ready, b + 1)
                pe.wait_ge(wv_split, 2)
                for t in range(ST):
                    tt = slice(t * P, (t + 1) * P)
                    for w in range(WC):
                        n = t * WC + w
                        if n >= 2:
                            pe.wait_ge(v_copied, b * (ST * WC) + (n - 1))
                        elif n == 0:
                            pe.wait_ge(resid_ready, b * NC + 1)
                        out, cols = sc[1][:, w % 2, :], slice(w * CH, (w + 1) * CH)
                        mm(out, xbh[:, tt], wvh[:, cols], start=True, stop=False)
                        mm(out, xbh[:, tt], wvl[:, cols], start=False, stop=False)
                        mm(out, xbl[:, tt], wvh[:, cols], start=False, stop=True).then_inc(v_ready, 1)
                with pe.Fori(0, NP // 2) as ppq:
                    pp = ppq * 2
                    for j in range(2):
                        u = b * NP + pp + j
                        for s in range(NS):
                            if (j, s) == (0, 1):
                                pe.wait_ge(v_copied, b * (ST * WC) + ST * WC)
                            parts = [scores(u, s, j)] * 2 + [values(u, s - 1, j, b, pp + j)] * 2 if s else [iter([None])]
                            own = list(enumerate(slots[s], begin[s]))
                            for i, part in enumerate(parts):
                                next(part)
                                for n, x in own[len(own) * i // len(parts):len(own) * (i + 1) // len(parts)]:
                                    job(u + 1, 1 - j, n, x, loop_count(u))
                        for n, x in enumerate(slots[NS][:-1], begin[NS]):
                            job(u + 1, 1 - j, n, x, loop_count(u))
                        for _ in values(u, NS - 1, j, b, pp + j):
                            pass
                        for _ in scores(u + 1, 0, 1 - j):
                            pass
                        job(u + 1, 1 - j, NL - 1, SUM0, loop_count(u))
                for done, pairs in ((NP - 1, range(NP - 1)), (NP, (NP - 1,))):
                    pe.wait_ge(z_ready, b * (NP * NC) + (done * NC + 2))
                    for k in range(NC):
                        for p in pairs:
                            last = mm(sc[1][:, k, :], wo_sb[:, p, :], VZ[:, p, k * CH:(k + 1) * CH], start=p == 0,
                                      stop=p == NP - 1)
                        if done == NP:
                            last.then_inc(o_ready, 1)
                for k in range(NC):
                    pe.wait_ge(ob_ready, b * NC + (k + 1))
                    for t in range(QT):
                        last = nc.tensor.transpose(outT[k][:, t * P:(t + 1) * P], oT[k][:, t * P:(t + 1) * P],
                                                   g.ident[:])
                    last.then_inc(ot_ready, 1)


def store(nc, g, out):
    with ExitStack() as st:
        c = Ctx(nc, st)
        stored = c.sem("stored")
        block = st.enter_context(nc.Block())

        @block.sync
        def _(sp):
            sp.dma_start(out.rearrange("b (t p) d -> p (b t) d", p=P), g.resid[:]).then_inc(stored, 16)
            sp.wait_ge(stored, 16)


def macaron(nc, x, W_Q, W_K, W_V, W_out, b_out, Wg, W1, b1, W2, b2, Ws1, bs1, Ws2, bs2, out, stages=(0, 1, 2)):
    B, S, D = x.shape
    E = Wg.shape[1]
    T = B * S // P
    with ExitStack() as st:
        g = Ctx(nc, st)
        g.n = "g"
        g.resid = g.sb("resid", [P, T, D])
        g.stats = g.sb("stats", [P, T, 6])
        g.xh, g.xl = g.sb("xh", [P, B * S], F32R), g.sb("xl", [P, B * S], F32R)
        g.ident, g.ident_b = g.sb("ident", [P, P]), g.sb("ident_b", [P, P], BF16)
        g.mask = g.sb("mask", [P, P], BF16)
        g.ones, g.eps = g.sb("ones", [P, W_Q.shape[2]]), g.sb("eps", [P, 1])
        g.rank_i, g.rank = g.sb("rank_i", [P, E], mybir.dt.int32), g.sb("rank", [P, E])
        g.stage = 0
        load_constants(nc, g, x)
        for layer in stages:
            g.stage = layer
            if layer == 1:
                layernorm(nc, g, layer == stages[0])
                attention(nc, g, W_Q, W_K, W_V, W_out, b_out, S, layer != stages[-1])
            else:
                with ExitStack() as inner:
                    c = Ctx(nc, inner)
                    c.n = layer
                    g.cwT, g.select = c.sb("cwT", [P, B * S], F32R), c.sb("select", [P, E, P], F32R)
                    weights = ExpertWeights(c, W1, b1, W2, b2, Ws1, bs1, Ws2, bs2)
                    layernorm(nc, g, layer == stages[0], Wg, weights)
                    moe(nc, g, weights, layer != stages[-1])
        store(nc, g, out)


_INS = ["L0_attn_resid", "L0_attn_W_Q", "L0_attn_W_K", "L0_attn_W_V", "L0_attn_W_out", "L0_attn_b_out", "L0_ffn_Wg",
        "L0_ffn_W1", "L0_ffn_b1", "L0_ffn_W2", "L0_ffn_b2", "L0_ffn_Ws1", "L0_ffn_bs1", "L0_ffn_Ws2", "L0_ffn_bs2"]


def kernel(**inputs):
    import numpy as _np
    import concourse.bacc as _bacc
    from concourse import mybir as _mybir
    from concourse.bass_utils import run_bass_kernel_spmd as _run

    nc = _bacc.Bacc("TRN2", target_bir_lowering=False, num_devices=1)
    arrays, args = {}, []
    for name in _INS:
        a = _np.ascontiguousarray(inputs[name])
        arrays[f"in_{name}"] = a
        args.append(nc.dram_tensor(f"in_{name}", a.shape, _mybir.dt.from_np(a.dtype), kind="ExternalInput").ap())
    out = nc.dram_tensor("out_x", arrays["in_L0_attn_resid"].shape, _mybir.dt.float32, kind="ExternalOutput").ap()
    macaron(nc, *args, out)
    r = _run(nc, [arrays], core_ids=[0])
    return r.results[0]["out_x"]
```
